# Optimizing a Trainium2 kernel written in Bass

```python
import numpy as np
import jax
import jax.numpy as jnp

def _softmax(x, axis=-1):
    return jax.nn.softmax(x, axis=axis)

def _gelu(x):
    return jax.nn.gelu(x, approximate=True)

def _silu(x):
    return jax.nn.silu(x)

def _sigmoid(x):
    return jax.nn.sigmoid(x)

def _layernorm(x, axis=-1, eps=1e-05):
    m = jnp.mean(x, axis=axis, keepdims=True)
    v = jnp.var(x, axis=axis, keepdims=True)
    return (x - m) / jnp.sqrt(v + eps)

def _scatter_add(tgt, idx, src, axis=0):
    return tgt.at[idx].add(src)

def _segment_sum(src, seg, n):
    return jax.ops.segment_sum(src, seg, n)
kernel_name = 'mk_recurrent_d2_jaxref_r8_087052'

def setup_inputs(seed: int=0):
    np.random.seed(seed)
    _w = jnp.asarray

    def _L0_attn_setup():
        import jax, jax.numpy as jnp
        import numpy as np
        B, T, D = (8, 512, 128)
        key = jax.random.key(seed)
        k1, k2, k3, k4, k5 = jax.random.split(key, 5)
        s = 1.0 / np.sqrt(D)
        return {'seq': jax.random.normal(k1, (B, T, D), dtype=jnp.float32), 'W_delta': jax.random.uniform(k2, (D, D), jnp.float32, -s, s), 'b_delta': jax.random.uniform(k3, (D,), jnp.float32, -s, s), 'W_value': jax.random.uniform(k4, (D, D), jnp.float32, -s, s), 'b_value': jax.random.uniform(k5, (D,), jnp.float32, -s, s)}
    _L0_attn_in = _L0_attn_setup()

    def _L0_ffn_setup():
        import jax, jax.numpy as jnp
        import numpy as np
        THRESH_FACTOR = 0.7

        def ternary_quantize(w):
            delta = THRESH_FACTOR * jnp.mean(jnp.abs(w))
            return jnp.where(w > delta, 1.0, jnp.where(w < -delta, -1.0, 0.0)).astype(w.dtype)
        key = jax.random.key(seed)
        k1, k2, k3 = jax.random.split(key, 3)
        B, S, D_IN, D_OUT = (8, 512, 128, 128)
        inp = {'input': jax.random.normal(k1, (B, S, D_IN), dtype=jnp.float32), 'weight': jax.random.normal(k2, (D_OUT, D_IN), dtype=jnp.float32) * (1.0 / np.sqrt(D_IN)), 'alpha': jnp.ones((1,), dtype=jnp.float32), 'bias': jax.random.normal(k3, (D_OUT,), dtype=jnp.float32) * (1.0 / np.sqrt(D_IN))}
        return inp
    _L0_ffn_in = _L0_ffn_setup()

    def _L1_attn_setup():
        import jax, jax.numpy as jnp
        import numpy as np
        import math
        HIDDEN = 128
        HEADS = 8
        HEAD = HIDDEN // HEADS
        B, S = (2, 256)
        SCALE_BASE = 64
        EPS = 1e-05

        def _xpos(x, downscale=False):
            d = x.shape[-1]
            s = x.shape[-2]
            half = d // 2
            scale_vec = (jnp.arange(0, d, 2, dtype=jnp.float32) + 0.4 * d) / (1.4 * d)
            pos = jnp.arange(s, dtype=jnp.float32)
            scale = scale_vec[None, :] ** (pos[:, None] / SCALE_BASE)
            inv_freq = 1.0 / 10000.0 ** (jnp.arange(half, dtype=jnp.float32) / half)
            ang = pos[:, None] * inv_freq[None, :]
            sin, cos = (jnp.sin(ang), jnp.cos(ang))
            if downscale:
                scale = 1.0 / scale
            sinp = jnp.repeat(sin * scale, 2, axis=-1)
            cosp = jnp.repeat(cos * scale, 2, axis=-1)
            x1, x2 = (x[..., ::2], x[..., 1::2])
            rot = jnp.stack([-x2, x1], axis=-1).reshape(x.shape)
            return x * cosp + rot * sinp

        def _gammas(h):
            return 1.0 - jnp.exp(jnp.linspace(math.log(1.0 / 32), math.log(1.0 / 64), h)).astype(jnp.float32)
        key = jax.random.key(seed)
        ks = jax.random.split(key, 6)
        X = jax.random.normal(ks[0], (B, S, HIDDEN), dtype=jnp.float32)
        W_Q = jax.random.normal(ks[1], (HEADS, HIDDEN, HEAD), dtype=jnp.float32) / HIDDEN
        W_K = jax.random.normal(ks[2], (HEADS, HIDDEN, HEAD), dtype=jnp.float32) / HIDDEN
        W_V = jax.random.normal(ks[3], (HEADS, HIDDEN, HEAD), dtype=jnp.float32) / HIDDEN
        W_G = jax.random.normal(ks[4], (HIDDEN, HIDDEN), dtype=jnp.float32) / HIDDEN
        W_O = jax.random.normal(ks[5], (HIDDEN, HIDDEN), dtype=jnp.float32) / HIDDEN
        gn_weight = jnp.ones((HIDDEN,), dtype=jnp.float32)
        gn_bias = jnp.zeros((HIDDEN,), dtype=jnp.float32)
        return dict(X=X, W_Q=W_Q, W_K=W_K, W_V=W_V, W_G=W_G, W_O=W_O, gn_weight=gn_weight, gn_bias=gn_bias)
    _L1_attn_in = _L1_attn_setup()

    def _L1_ffn_setup():
        import jax, jax.numpy as jnp
        import numpy as np
        D_MODEL = 128
        N_EXPERTS = 8
        TOP_K = 2
        BOTTLENECK = 64
        B, S = (2, 512)
        ADAPTER_SCALE = 0.5

        def _moe_forward(x, w_gate, w_noise, Wd, bd, Wu, bu):
            b, s, d = x.shape
            xf = x.reshape(-1, d)
            T = xf.shape[0]
            clean_logits = xf @ w_gate
            logits = clean_logits
            k1 = min(TOP_K + 1, N_EXPERTS)
            top_logits, top_idx = jax.lax.top_k(logits, k1)
            top_k_logits = top_logits[:, :TOP_K]
            top_k_idx = top_idx[:, :TOP_K]
            top_k_gates = jax.nn.softmax(top_k_logits, axis=-1)
            rows = jnp.arange(T)[:, None]
            gates = jnp.zeros((T, N_EXPERTS), dtype=top_k_gates.dtype)
            gates = gates.at[rows, top_k_idx].set(top_k_gates)
            h = jax.nn.relu(jnp.einsum('td,edb->teb', xf, Wd) + bd[None, :, :])
            y = jnp.einsum('teb,ebd->ted', h, Wu) + bu[None, :, :]
            y = ADAPTER_SCALE * y
            out = jnp.einsum('te,ted->td', gates, y)
            return out.reshape(b, s, d)
        key = jax.random.key(seed)
        ks = jax.random.split(key, 8)
        sd = 0.02
        x = jax.random.normal(ks[0], (B, S, D_MODEL), dtype=jnp.float32)
        w_gate = jax.random.normal(ks[1], (D_MODEL, N_EXPERTS), dtype=jnp.float32) * sd
        w_noise = jax.random.normal(ks[2], (D_MODEL, N_EXPERTS), dtype=jnp.float32) * sd
        Wd = jax.random.normal(ks[3], (N_EXPERTS, D_MODEL, BOTTLENECK), dtype=jnp.float32) * sd
        bd = jnp.zeros((N_EXPERTS, BOTTLENECK), dtype=jnp.float32)
        Wu = jax.random.normal(ks[4], (N_EXPERTS, BOTTLENECK, D_MODEL), dtype=jnp.float32) * sd
        bu = jnp.zeros((N_EXPERTS, D_MODEL), dtype=jnp.float32)
        return {'x': x, 'w_gate': w_gate, 'w_noise': w_noise, 'Wd': Wd, 'bd': bd, 'Wu': Wu, 'bu': bu}
    _L1_ffn_in = _L1_ffn_setup()
    _d = {'L0_attn_seq': _L0_attn_in['seq'], 'L0_attn_W_delta': _L0_attn_in['W_delta'], 'L0_attn_b_delta': _L0_attn_in['b_delta'], 'L0_attn_W_value': _L0_attn_in['W_value'], 'L0_attn_b_value': _L0_attn_in['b_value'], 'L0_ffn_weight': _L0_ffn_in['weight'], 'L0_ffn_alpha': _L0_ffn_in['alpha'], 'L0_ffn_bias': _L0_ffn_in['bias'], 'L1_attn_W_Q': _L1_attn_in['W_Q'], 'L1_attn_W_K': _L1_attn_in['W_K'], 'L1_attn_W_V': _L1_attn_in['W_V'], 'L1_attn_W_G': _L1_attn_in['W_G'], 'L1_attn_W_O': _L1_attn_in['W_O'], 'L1_attn_gn_weight': _L1_attn_in['gn_weight'], 'L1_attn_gn_bias': _L1_attn_in['gn_bias'], 'L1_ffn_w_gate': _L1_ffn_in['w_gate'], 'L1_ffn_w_noise': _L1_ffn_in['w_noise'], 'L1_ffn_Wd': _L1_ffn_in['Wd'], 'L1_ffn_bd': _L1_ffn_in['bd'], 'L1_ffn_Wu': _L1_ffn_in['Wu'], 'L1_ffn_bu': _L1_ffn_in['bu']}
    _x0 = _d['L0_attn_seq']
    _d['L0_attn_seq'] = jax.random.normal(jax.random.fold_in(jax.random.key(seed), 1), (2, 1024, 128), dtype=_x0.dtype)
    del _x0
    return _d

def reference(L0_attn_seq, L0_attn_W_delta, L0_attn_b_delta, L0_attn_W_value, L0_attn_b_value, L0_ffn_weight, L0_ffn_alpha, L0_ffn_bias, L1_attn_W_Q, L1_attn_W_K, L1_attn_W_V, L1_attn_W_G, L1_attn_W_O, L1_attn_gn_weight, L1_attn_gn_bias, L1_ffn_w_gate, L1_ffn_w_noise, L1_ffn_Wd, L1_ffn_bd, L1_ffn_Wu, L1_ffn_bu):

    def _L0_attn_ref(seq, W_delta, b_delta, W_value, b_value):
        import jax, jax.numpy as jnp
        import numpy as np
        B, T, D = (8, 512, 128)
        delta = jax.nn.sigmoid(jnp.einsum('btd,ed->bte', seq, W_delta) + b_delta)
        value = jnp.einsum('btd,ed->bte', seq, W_value) + b_value

        def step(state, dv):
            d, v = dv
            state = (1.0 - d) * state + d * v
            return (state, state)
        init = jnp.zeros((seq.shape[0], seq.shape[-1]), dtype=seq.dtype)
        _, out = jax.lax.scan(step, init, (delta.transpose(1, 0, 2), value.transpose(1, 0, 2)))
        return out.transpose(1, 0, 2)

    def _L0_ffn_ref(input, weight, alpha, bias):
        import jax, jax.numpy as jnp
        import numpy as np
        THRESH_FACTOR = 0.7

        def ternary_quantize(w):
            delta = THRESH_FACTOR * jnp.mean(jnp.abs(w))
            return jnp.where(w > delta, 1.0, jnp.where(w < -delta, -1.0, 0.0)).astype(w.dtype)
        w_ternary = ternary_quantize(weight)
        w_eff = w_ternary * alpha
        out = jnp.einsum('bsd,od->bso', input, w_eff) + bias
        return out

    def _L1_attn_ref(X, W_Q, W_K, W_V, W_G, W_O, gn_weight, gn_bias):
        import jax, jax.numpy as jnp
        import numpy as np
        import math
        HIDDEN = 128
        HEADS = 8
        HEAD = HIDDEN // HEADS
        B, S = (2, 256)
        SCALE_BASE = 64
        EPS = 1e-05

        def _xpos(x, downscale=False):
            d = x.shape[-1]
            s = x.shape[-2]
            half = d // 2
            scale_vec = (jnp.arange(0, d, 2, dtype=jnp.float32) + 0.4 * d) / (1.4 * d)
            pos = jnp.arange(s, dtype=jnp.float32)
            scale = scale_vec[None, :] ** (pos[:, None] / SCALE_BASE)
            inv_freq = 1.0 / 10000.0 ** (jnp.arange(half, dtype=jnp.float32) / half)
            ang = pos[:, None] * inv_freq[None, :]
            sin, cos = (jnp.sin(ang), jnp.cos(ang))
            if downscale:
                scale = 1.0 / scale
            sinp = jnp.repeat(sin * scale, 2, axis=-1)
            cosp = jnp.repeat(cos * scale, 2, axis=-1)
            x1, x2 = (x[..., ::2], x[..., 1::2])
            rot = jnp.stack([-x2, x1], axis=-1).reshape(x.shape)
            return x * cosp + rot * sinp

        def _gammas(h):
            return 1.0 - jnp.exp(jnp.linspace(math.log(1.0 / 32), math.log(1.0 / 64), h)).astype(jnp.float32)
        b, s, _ = X.shape
        h, _, dv = W_V.shape
        Q = _xpos(jnp.einsum('bse,hed->bhsd', X, W_Q))
        K = _xpos(jnp.einsum('bse,hed->bhsd', X, W_K), downscale=True)
        V = jnp.einsum('bse,hed->bhsd', X, W_V)
        gam = _gammas(h)
        n = jnp.arange(s)
        diff = n[:, None] - n[None, :]
        mask = diff >= 0
        D = jnp.where(mask[None], gam[:, None, None] ** jnp.where(mask, diff, 0)[None].astype(jnp.float32), 0.0)
        scores = jnp.einsum('bhsd,bhtd->bhst', Q, K) * D[None]
        Y = jnp.einsum('bhst,bhtv->bhsv', scores, V)
        Y = jnp.transpose(Y, (0, 2, 1, 3))
        mu = Y.mean(-1, keepdims=True)
        var = Y.var(-1, keepdims=True)
        Yn = ((Y - mu) / jnp.sqrt(var + EPS)).reshape(b, s, h * dv) * gn_weight + gn_bias
        gate = X @ W_G
        gate = gate * jax.nn.sigmoid(gate)
        return gate * Yn @ W_O

    def _L1_ffn_ref(x, w_gate, w_noise, Wd, bd, Wu, bu):
        import jax, jax.numpy as jnp
        import numpy as np
        D_MODEL = 128
        N_EXPERTS = 8
        TOP_K = 2
        BOTTLENECK = 64
        B, S = (2, 512)
        ADAPTER_SCALE = 0.5

        def _moe_forward(x, w_gate, w_noise, Wd, bd, Wu, bu):
            b, s, d = x.shape
            xf = x.reshape(-1, d)
            T = xf.shape[0]
            clean_logits = xf @ w_gate
            logits = clean_logits
            k1 = min(TOP_K + 1, N_EXPERTS)
            top_logits, top_idx = jax.lax.top_k(logits, k1)
            top_k_logits = top_logits[:, :TOP_K]
            top_k_idx = top_idx[:, :TOP_K]
            top_k_gates = jax.nn.softmax(top_k_logits, axis=-1)
            rows = jnp.arange(T)[:, None]
            gates = jnp.zeros((T, N_EXPERTS), dtype=top_k_gates.dtype)
            gates = gates.at[rows, top_k_idx].set(top_k_gates)
            h = jax.nn.relu(jnp.einsum('td,edb->teb', xf, Wd) + bd[None, :, :])
            y = jnp.einsum('teb,ebd->ted', h, Wu) + bu[None, :, :]
            y = ADAPTER_SCALE * y
            out = jnp.einsum('te,ted->td', gates, y)
            return out.reshape(b, s, d)
        return _moe_forward(x, w_gate, w_noise, Wd, bd, Wu, bu)
    x = L0_attn_seq
    xn = _layernorm(x, axis=-1)
    s = _L0_attn_ref(xn, L0_attn_W_delta, L0_attn_b_delta, L0_attn_W_value, L0_attn_b_value)
    g = _silu(_L0_ffn_ref(xn, L0_ffn_weight, L0_ffn_alpha, L0_ffn_bias))
    x = x + s * g
    xn = _layernorm(x, axis=-1)
    s = _L1_attn_ref(xn, L1_attn_W_Q, L1_attn_W_K, L1_attn_W_V, L1_attn_W_G, L1_attn_W_O, L1_attn_gn_weight, L1_attn_gn_bias)
    g = _silu(_L1_ffn_ref(xn, L1_ffn_w_gate, L1_ffn_w_noise, L1_ffn_Wd, L1_ffn_bd, L1_ffn_Wu, L1_ffn_bu))
    x = x + s * g
    return x

_drawn_inputs = setup_inputs


def setup_inputs(seed=0):
    import zlib

    import numpy as np

    out = dict(_drawn_inputs(seed))
    spreads = {'L1_attn_gn_weight': (1.0, 0.6),
     'L1_attn_gn_bias': (0.0, 0.8),
     'L1_ffn_bd': (0.0, 2.0),
     'L1_ffn_bu': (0.0, 2.0)}
    factors = {'L0_attn_b_delta': 4.136,
     'L0_ffn_bias': 6.988,
     'L1_attn_W_Q': 8.0,
     'L1_attn_W_K': 8.0,
     'L1_attn_W_V': 8.0,
     'L1_attn_W_G': 8.0,
     'L1_attn_W_O': 8.0,
     'L1_ffn_w_gate': 8.0,
     'L1_ffn_Wd': 8.0,
     'L1_ffn_Wu': 8.0}
    for name, (base, spread) in spreads.items():
        noise = np.random.default_rng([zlib.crc32(name.encode()), seed]).standard_normal(out[name].shape)
        drawn = base * np.exp(spread * noise) if base else spread * noise
        out[name] = jnp.asarray(drawn.astype(out[name].dtype))
    for name, factor in factors.items():
        out[name] = (out[name] * factor).astype(out[name].dtype)
    return out
```

```python
from contextlib import ExitStack

import numpy as np
import concourse.bass as bass
from concourse import mybir

F32 = mybir.dt.float32
ALU = mybir.AluOpType
ACT = mybir.ActivationFunctionType
AX = mybir.AxisListType

P = 128
BATCH, SEQ, DIM = 2, 1024, 128
PAIRS = SEQ // P
HEADS, HEAD = 8, 16
CHUNK = 64
CHUNKS = P // CHUNK
STRIPES = 4
EXPERTS, NECK = 8, 64
DOWN = EXPERTS * NECK // P
EPS = 1e-5
LAG = 2
PEEL = 3

W_PARTS = [("delta", DIM), ("value", DIM), ("ffn", DIM), ("b_delta", 1), ("b_value", 1), ("b_ffn", 1),
           ("alpha", 1)]
V_PARTS = [("qk", 2 * DIM), ("v", DIM), ("g", DIM), ("logit", EXPERTS), ("o", DIM),
           ("down", EXPERTS * NECK), ("up", DOWN * DIM), ("b_down", DOWN), ("b_up", DIM),
           ("gn_w", DIM), ("gn_b", DIM)]
C_PARTS = [("identity", P), ("causal", CHUNK), ("same_head", DIM), ("even_head", 1), ("odd_head", 1), ("own_heads", DIM),
           ("descending", BATCH * EXPERTS)]


def columns(parts):
    at, out = 0, {}
    for name, n in parts:
        out[name] = (at, at + n)
        at += n
    return out, at


W_AT, W_N = columns(W_PARTS)
V_AT, V_N = columns(V_PARTS)
C_AT, C_N = columns(C_PARTS)


def constants():
    c = np.zeros((P, C_N), np.float32)
    r = np.arange(P)
    put = lambda name, a: c.__setitem__((slice(None), slice(*C_AT[name])), a)
    put("identity", np.eye(P))
    put("causal", np.arange(CHUNK)[None, :] >= (r % CHUNK)[:, None])
    put("same_head", (r // HEAD)[:, None] == (np.arange(DIM) // HEAD)[None, :])
    put("even_head", (r // HEAD % 2 == 0)[:, None])
    put("odd_head", (r // HEAD % 2 == 1)[:, None])
    put("own_heads", (r // 64)[:, None] == (np.arange(DIM) // HEAD % 2)[None, :])
    put("descending", np.tile(np.arange(EXPERTS, 0, -1), BATCH)[None, :])
    f = np.float32
    half = HEAD // 2
    scale = (np.arange(0, HEAD, 2, dtype=f) + f(0.4 * HEAD)) / f(1.4 * HEAD)
    gamma = (1.0 - np.exp(np.linspace(np.log(1 / 32), np.log(1 / 64), HEADS))).astype(f)
    pos = np.arange(SEQ, dtype=f)
    freq = (f(1.0) / f(10000.0) ** (np.arange(half, dtype=f) / f(half))).astype(f)
    angle = (pos[:, None] * freq[None, :]).astype(f).astype(np.float64)
    mid = pos.astype(np.float64) - SEQ // 2
    grow = (scale.astype(np.float64)[None, None, :] ** (mid[:, None, None] / 64.0)
            * gamma.astype(np.float64)[None, :, None] ** mid[:, None, None])
    both = np.stack([grow, 1.0 / grow], 1)
    tables = np.stack([both * np.cos(angle)[:, None, None, :], both * np.sin(angle)[:, None, None, :]], 1)
    tables = tables.reshape(PAIRS, P, 2, DIM).transpose(1, 0, 2, 3)
    return c, np.ascontiguousarray(tables.astype(f))


def two_layers(nc, x, w0, w1, const, tables, gate_rows, out):
    with ExitStack() as ctx:
        def sb(name, *shape):
            return ctx.enter_context(nc.sbuf_tensor(name, [P, *shape], F32))

        def sem(name):
            return ctx.enter_context(nc.semaphore(name))

        x_sb = sb("x_sb", BATCH, PAIRS, DIM)
        x1_sb = sb("x1_sb", BATCH, PAIRS, DIM)
        out_sb = sb("out_sb", BATCH, PAIRS, DIM)
        tab = sb("tab", PAIRS, 2, DIM)
        w0_sb = sb("w0_sb", W_N)
        w1_sb = sb("w1_sb", V_N)
        c_sb = sb("c_sb", C_N)
        W = {k: w0_sb[:, a:b] for k, (a, b) in W_AT.items()}
        V = {k: w1_sb[:, a:b] for k, (a, b) in V_AT.items()}
        C = {k: c_sb[:, a:b] for k, (a, b) in C_AT.items()}
        abs_sum = sb("abs_sum", 1)
        ones = sb("ones", P)
        zeros = sb("zeros", BATCH * DIM)
        threshold = sb("threshold", 2)
        above = sb("above", DIM)
        below = sb("below", DIM)
        w_tern = sb("w_tern", DIM)
        neg_b_delta = sb("neg_b_delta", 1)
        neg_half = sb("neg_half", BATCH * HEADS)
        stats0 = sb("stats0", BATCH, 6)
        moments0 = sb("moments0", BATCH, 2)
        var0 = sb("var0", BATCH)
        rstd0 = sb("rstd0", BATCH)
        xn0 = sb("xn0", BATCH, DIM)
        xn0T = sb("xn0T", BATCH * P)
        keep = sb("keep", BATCH * P)
        delta = sb("delta", BATCH * P)
        sig_ffn = sb("sig_ffn", BATCH * P)
        drive = sb("drive", BATCH * P)
        carry = sb("carry", BATCH)
        scan = sb("scan", BATCH, P)
        ffn_silu = sb("ffn_silu", BATCH * P)
        gated0 = sb("gated0", BATCH * P)
        stats1 = sb("stats1", BATCH, 6)
        moments1 = sb("moments1", BATCH, 2)
        var1 = sb("var1", BATCH)
        rstd1 = sb("rstd1", BATCH)
        xn1 = sb("xn1", BATCH, DIM)
        xn1T = sb("xn1T", BATCH * P)
        by_cos = sb("by_cos", BATCH, 2 * DIM)
        by_sin = sb("by_sin", BATCH, 2 * DIM)
        qk = sb("qk", BATCH, 2, DIM)
        v_twice = sb("v_twice", BATCH, CHUNKS, DIM)
        v_split = sb("v_split", BATCH, CHUNKS, DIM)
        qT = sb("qT", BATCH * P)
        kT = sb("kT", BATCH, CHUNKS, 2, CHUNK)
        sig_g = sb("sig_g", BATCH * DIM)
        g_silu = sb("g_silu", BATCH, DIM)
        g_w = sb("g_w", BATCH, DIM)
        g_b = sb("g_b", BATCH, DIM)
        logits = sb("logits", BATCH, EXPERTS)
        top1 = sb("top1", BATCH)
        top2 = sb("top2", BATCH)
        is_top = sb("is_top", BATCH, EXPERTS)
        first_at = sb("first_at", BATCH)
        hot1 = sb("hot1", BATCH, EXPERTS)
        rest = sb("rest", BATCH, EXPERTS)
        hot2 = sb("hot2", BATCH, EXPERTS)
        margin = sb("margin", BATCH)
        share1 = sb("share1", BATCH)
        share2 = sb("share2", BATCH)
        gates = sb("gates", BATCH, EXPERTS)
        gatesT = sb("gatesT", BATCH * P)
        gate_wide = sb("gate_wide", DOWN, BATCH * P)
        hidden = sb("hidden", DOWN, BATCH * P)
        gated_h = sb("gated_h", DOWN, BATCH * P)
        masked = sb("masked", STRIPES, BATCH, CHUNKS, CHUNK)
        state_a = sb("state_a", BATCH, DIM)
        state_b = sb("state_b", BATCH, DIM)
        y_sum = sb("y_sum", BATCH * HEADS)
        y_mid = sb("y_mid", BATCH * HEADS, HEAD)
        y_sq = sb("y_sq", BATCH * HEADS, HEAD)
        y_var = sb("y_var", BATCH * HEADS)
        y_vare = sb("y_vare", BATCH * HEADS)
        y_rstd = sb("y_rstd", BATCH * HEADS)
        y_norm = sb("y_norm", BATCH * HEADS, HEAD)
        y_w = sb("y_w", BATCH, DIM)
        gated_y = sb("gated_y", BATCH, DIM)
        gated_yT = sb("gated_yT", BATCH * P)
        sig_moe = sb("sig_moe", BATCH * DIM)
        moe_silu = sb("moe_silu", BATCH * DIM)
        update = sb("update", BATCH, DIM)

        ps = ctx.enter_context(nc.psum_tensor("ps", [P, 8, 512], F32))
        bank_t = ps[:, 0, 0:256]
        bank_dv = ps[:, 1, :]
        bank_f = ps[:, 2, :]
        bank_qk = ps[:, 3, :]
        bank_v = ps[:, 4, :]
        bank_qkT = ps[:, 5, :]
        bank_y = ps[:, 6, 0:256]
        bank_s = ps[:, 7, 0:256]
        scores = ps[:, 3:7, 0:256]

        names = """x_first x_rest w0_in w1_in const_in tab_in ones_set zeros_set carry_set state_set
            neg_half_set abs_sum_r abs_total threshold_m threshold_r above_r below_r tern_sign tern_r neg_b_r
            stats0_r moments0_r var0_r rstd0_r xn0_r xn0_T xn0T_r dv_z ffn_z keep_r delta_r sig_ffn_r drive_r
            scan_r carry_r ffn_silu_r gated0_r gated0_T x1_r stats1_r moments1_r var1_r rstd1_r xn1_r xn1_T
            xn1T_r qk_z v_z g_z rot1_r rot2_r qk_r v_twice_r v_split_r qk_T qT_r kT_r sig_g_r g_silu_r g_w_r
            g_b_r logits_r top1_r istop1_r firstkey1_r first1_r hot1_r rest_r top2_r istop2_r firstkey2_r
            first2_r hot2_r margin_r share1_r share2_r part1_r part2_r gates_r gates_T gatesT_r gate_rows_w
            gate_wide_in down_z0 down_z1 hidden_r0 hidden_r1 gated_h_r moe_z scores_z masked_r state_k0
            state_b_r state_k1 state_a_r y_z y_sum_r y_mid_r y_sq_r y_var_r y_vare_r y_rstd_r y_norm_r y_w_r
            gated_y_r gated_y_T gated_yT_r ret_z sig_moe_r moe_silu_r update_r out_r out_w""".split()
        S = {n: sem(n) for n in names}

        def live(p):
            return not isinstance(p, int) or 0 <= p < PAIRS

        def first(p):
            return isinstance(p, int) and p == 0

        def all_steps(engine, step):
            for s in range(PEEL):
                step(s)
            with engine.Fori(PEEL + 1, PAIRS + 1) as done:
                step(done - 1)
            for s in range(PAIRS, PAIRS + LAG):
                step(s)

        def pair(buffer, b, p):
            return buffer[:, b, p, :] if isinstance(p, int) else buffer[:, b, bass.ds(p, 1), :]

        def both(buffer, p):
            return buffer[:, :, p, :] if isinstance(p, int) else buffer[:, :, bass.ds(p, 1), :]

        block = ctx.enter_context(nc.Block())

        @block.sync
        def _(sp):
            x_in = x.rearrange("b (p t) d -> t b p d", t=P)
            sp.dma_start(x_sb[:, :, 0:1, :], x_in[:, :, 0:1, :]).then_inc(S["x_first"], 16)
            sp.dma_start(w0_sb[:], w0).then_inc(S["w0_in"], 16)
            sp.dma_start(x_sb[:, 0, 1:PAIRS, :], x_in[:, 0, 1:PAIRS, :]).then_inc(S["x_rest"], 16)
            sp.dma_start(x_sb[:, 1, 1:PAIRS, :], x_in[:, 1, 1:PAIRS, :]).then_inc(S["x_rest"], 16)
            sp.dma_start(w1_sb[:], w1).then_inc(S["w1_in"], 16)
            sp.dma_start(tab[:], tables).then_inc(S["tab_in"], 16)

            def spread_gates(p):
                sp.wait_ge(S["gatesT_r"], p + 1)
                if not first(p):
                    sp.wait_ge(S["gate_wide_in"], p * 32)
                sp.dma_start(gate_rows, gatesT[0:EXPERTS, :]).then_inc(S["gate_rows_w"], 16)
                sp.wait_ge(S["gate_rows_w"], p * 16 + 16)
                if not first(p):
                    sp.wait_ge(S["gated_h_r"], p)
                rows = gate_rows.rearrange("(c h) t -> h c t", h=2)
                for h in range(2):
                    src = rows[h].rearrange("(o c) t -> o c t", o=1).to_broadcast([NECK, DOWN, BATCH * P])
                    sp.dma_start(gate_wide[NECK * h:NECK * (h + 1)], src).then_inc(S["gate_wide_in"], 16)

            def store(p):
                sp.wait_ge(S["out_r"], p + 1)
                o = out.rearrange("b (p t) d -> t b p d", t=P)
                for b in range(BATCH):
                    if isinstance(p, int):
                        dst = o[:, b, p, :]
                    else:
                        dst = o[:, b, bass.ds(p, 1), :]
                    sp.dma_start(dst, pair(out_sb, b, p)).then_inc(S["out_w"], 16)

            def step(s):
                if live(s - 1):
                    spread_gates(s - 1)
                if live(s - 2):
                    store(s - 2)

            all_steps(sp, step)
            sp.wait_ge(S["out_w"], 16 * BATCH * PAIRS)

        @block.tensor
        def _(pe):
            half = lambda b: slice(b * P, (b + 1) * P)
            pe.wait_ge(S["ones_set"], 1)
            pe.wait_ge(S["abs_sum_r"], 1)
            pe.matmul(bank_f[:, 0:1], ones[:], abs_sum[:], start=True, stop=True).then_inc(S["abs_total"], 1)
            pe.wait_ge(S["zeros_set"], 1)
            pe.matmul(bank_s, zeros[:, 0:P], zeros[:], start=True, stop=False, skip_group_check=True)
            pe.wait_ge(S["const_in"], 16)

            def turn_x(p):
                pe.wait_ge(S["xn0_r"], p + 1)
                if not first(p):
                    pe.wait_ge(S["xn1T_r"], p)
                if isinstance(p, int) and p >= 3 or not isinstance(p, int):
                    pe.wait_ge(S["gated_yT_r"], p - 2)
                for b in range(BATCH):
                    mm = pe.transpose(bank_t[:, half(b)], xn0[:, b, :], C["identity"])
                mm.then_inc(S["xn0_T"], 1)

            def project0(p):
                pe.wait_ge(S["xn0T_r"], p + 1)
                if first(p):
                    pe.wait_ge(S["w0_in"], 16)
                if isinstance(p, int) and p >= 3 or not isinstance(p, int):
                    pe.wait_ge(S["update_r"], p - 2)
                if not first(p):
                    pe.wait_ge(S["drive_r"], p)
                pe.matmul(bank_dv[:, 0:256], W["delta"], xn0T[:], start=True, stop=True)
                pe.matmul(bank_dv[:, 256:512], W["value"], xn0T[:], start=True, stop=True).then_inc(S["dv_z"], 1)
                if first(p):
                    pe.wait_ge(S["tern_r"], 1)
                if isinstance(p, int) and p >= 2 or not isinstance(p, int):
                    pe.wait_ge(S["gatesT_r"], p - 1)
                pe.matmul(bank_f[:, 0:256], w_tern[:], xn0T[:], start=True, stop=True).then_inc(S["ffn_z"], 1)

            def turn_gated0(p):
                pe.wait_ge(S["gated0_r"], p + 1)
                for b in range(BATCH):
                    mm = pe.transpose(bank_t[:, half(b)], gated0[:, half(b)], C["identity"])
                mm.then_inc(S["gated0_T"], 1)

            def turn_x1(p):
                pe.wait_ge(S["xn1_r"], p + 1)
                for b in range(BATCH):
                    mm = pe.transpose(bank_t[:, half(b)], xn1[:, b, :], C["identity"])
                mm.then_inc(S["xn1_T"], 1)

            def project1(p):
                if first(p):
                    pe.wait_ge(S["w1_in"], 16)
                pe.wait_ge(S["xn1T_r"], p + 1)
                if not first(p):
                    pe.wait_ge(S["hidden_r1"], p)
                    pe.wait_ge(S["masked_r"], 2 * p)
                for b in range(BATCH):
                    mm = pe.matmul(bank_qk[:, b * 256:b * 256 + 256], xn1T[:, half(b)], V["qk"],
                                   start=True, stop=True)
                mm.then_inc(S["qk_z"], 1)
                for b in range(BATCH):
                    for k in range(CHUNKS):
                        at = b * P + k * CHUNK
                        for h in range(2):
                            mm = pe.matmul(bank_v[64 * h:64 * h + 64, (b * CHUNKS + k) * DIM:(b * CHUNKS + k + 1) * DIM],
                                           xn1T[:, at:at + CHUNK], V["v"], start=True, stop=True)
                mm.then_inc(S["v_z"], 1)
                if not (isinstance(p, int) and p == PAIRS - 1):
                    pe.wait_ge(S["ffn_silu_r"], p + 2)
                else:
                    pe.wait_ge(S["ffn_silu_r"], PAIRS)
                for b in range(BATCH):
                    pe.matmul(bank_f[:, half(b)], xn1T[:, half(b)], V["g"], start=True, stop=True)
                    mm = pe.matmul(bank_f[:, 256 + 8 * b:264 + 8 * b], xn1T[:, half(b)], V["logit"],
                                   start=True, stop=True)
                mm.then_inc(S["g_z"], 1)

            def turn_qk(p):
                pe.wait_ge(S["qk_r"], p + 1)
                for i in range(2):
                    for b in range(BATCH):
                        mm = pe.transpose(bank_qkT[:, (2 * i + b) * P:(2 * i + b + 1) * P], qk[:, b, i, :],
                                          C["identity"])
                mm.then_inc(S["qk_T"], 1)

            def experts_down(p):
                pe.wait_ge(S["gates_r"], p + 1)
                pe.wait_ge(S["g_silu_r"], p + 1)
                pe.wait_ge(S["logits_r"], p + 1)
                for b in range(BATCH):
                    mm = pe.transpose(bank_f[0:EXPERTS, half(b)], gates[:, b, :], C["identity"])
                mm.then_inc(S["gates_T"], 1)
                pe.wait_ge(S["rot2_r"], p + 1)
                for c in range(DOWN):
                    if c == 2:
                        pe.wait_ge(S["v_twice_r"], p + 1)
                    bank = (bank_qk, bank_v)[c // 2]
                    mm = pe.matmul(bank[:, (c % 2) * 256:(c % 2) * 256 + 256], V["down"][:, c * P:(c + 1) * P],
                                   xn1T[:], start=True, stop=True)
                    if c % 2:
                        mm.then_inc(S[f"down_z{c // 2}"], 1)

            def score(p):
                pe.wait_ge(S["qT_r"], p + 1)
                pe.wait_ge(S["kT_r"], p + 1)
                pe.wait_ge(S["hidden_r1"], p + 1)
                if not first(p):
                    pe.wait_ge(S["y_mid_r"], p)
                for b in range(BATCH):
                    for k in range(CHUNKS):
                        for i in range(STRIPES):
                            rows = slice(32 * i, 32 * i + 32)
                            at = b * P + k * CHUNK
                            mm = pe.matmul(scores[:, i, at:at + CHUNK], kT[rows, b, k, :, :], qT[rows, at:at + CHUNK],
                                           start=True, stop=True, tile_position=(32 * i, 0))
                mm.then_inc(S["scores_z"], 1)

            def retain(p):
                def add_to_state(k):
                    rows = slice(64 * k, 64 * k + 64)
                    for b in range(BATCH):
                        mm = pe.matmul(bank_s[:, b * DIM:(b + 1) * DIM], qk[rows, b, 1, :], v_twice[rows, b, k, :],
                                       start=False, stop=False, skip_group_check=True, tile_position=(64 * k, 0))
                    mm.then_inc(S[f"state_k{k}"], 1)

                def read_out(k):
                    rows = slice(64 * k, 64 * k + 64)
                    state = (state_a, state_b)[k]
                    for b in range(BATCH):
                        at = b * P + k * CHUNK
                        pe.matmul(bank_y[rows, b * DIM:(b + 1) * DIM], qT[:, at:at + CHUNK], state[:, b, :],
                                  start=True, stop=False, skip_group_check=True)
                        for i in range(STRIPES):
                            mm = pe.matmul(bank_y[rows, b * DIM + 32 * i:b * DIM + 32 * i + 32],
                                           masked[:, i, b, k, :], v_split[:, b, k, 32 * i:32 * i + 32],
                                           start=False, stop=(i == STRIPES - 1), skip_group_check=True)
                    return mm

                if not first(p):
                    pe.wait_ge(S["state_a_r"], p)
                else:
                    pe.wait_ge(S["state_set"], 1)
                pe.wait_ge(S["v_twice_r"], p + 1)
                add_to_state(0)
                pe.wait_ge(S["masked_r"], 2 * p + 2)
                pe.wait_ge(S["v_split_r"], p + 1)
                read_out(0)
                pe.wait_ge(S["state_b_r"], p + 1)
                add_to_state(1)
                read_out(1).then_inc(S["y_z"], 1)

            def experts_up(p):
                pe.wait_ge(S["gated_h_r"], p + 1)
                pe.wait_ge(S["drive_r"], min(p + 3, PAIRS) if isinstance(p, int) else p + 3)
                for b in range(BATCH):
                    o = bank_dv[:, 256 + b * DIM:256 + (b + 1) * DIM]
                    for c in range(DOWN):
                        pe.matmul(o, gated_h[:, c, half(b)], V["up"][:, c * DIM:(c + 1) * DIM],
                                  start=(c == 0), stop=False)
                    mm = pe.matmul(o, gatesT[0:EXPERTS, half(b)], V["b_up"][0:EXPERTS, :], start=False, stop=True)
                mm.then_inc(S["moe_z"], 1)

            def output(p):
                pe.wait_ge(S["gated_y_r"], p + 1)
                pe.wait_ge(S["xn1T_r"], min(p + 3, PAIRS) if isinstance(p, int) else p + 3)
                for b in range(BATCH):
                    mm = pe.transpose(bank_t[:, half(b)], gated_y[:, b, :], C["identity"])
                mm.then_inc(S["gated_y_T"], 1)
                pe.wait_ge(S["gated_yT_r"], p + 1)
                for b in range(BATCH):
                    mm = pe.matmul(bank_dv[:, b * DIM:(b + 1) * DIM], gated_yT[:, half(b)], V["o"],
                                   start=True, stop=True)
                mm.then_inc(S["ret_z"], 1)

            def step(s):
                a, b, c = s, s - 1, s - 2
                if live(a):
                    turn_x(a)
                if live(c):
                    score(c)
                if live(a):
                    project0(a)
                if live(c):
                    retain(c)
                if live(b):
                    project1(b)
                if live(a):
                    turn_gated0(a)
                if live(c):
                    experts_up(c)
                if live(b):
                    turn_qk(b)
                    experts_down(b)
                if live(a):
                    turn_x1(a)
                if live(c):
                    output(c)

            all_steps(pe, step)

        @block.scalar
        def _(act):
            act.dma_start(c_sb[:], const).then_inc(S["const_in"], 16)

            def norm0_out(p):
                act.wait_ge(S["xn0_T"], p + 1)
                if not first(p):
                    act.wait_ge(S["ffn_z"], p)
                act.copy(xn0T[:], bank_t).then_inc(S["xn0T_r"], 1)

            def sigmoids0(p):
                if first(p):
                    act.wait_ge(S["w0_in"], 16)
                    act.wait_ge(S["neg_b_r"], 1)
                act.wait_ge(S["dv_z"], p + 1)
                if not first(p):
                    act.wait_ge(S["drive_r"], p)
                act.activation(delta[:], bank_dv[:, 0:256], ACT.Sigmoid, bias=W["b_delta"]).then_inc(S["delta_r"], 1)
                if not first(p):
                    act.wait_ge(S["scan_r"], 2 * p)
                act.activation(keep[:], bank_dv[:, 0:256], ACT.Sigmoid, bias=neg_b_delta[:], scale=-1.0).then_inc(S["keep_r"], 1)
                act.wait_ge(S["ffn_z"], p + 1)
                if not first(p):
                    act.wait_ge(S["ffn_silu_r"], p)
                act.activation(sig_ffn[:], bank_f[:, 0:256], ACT.Sigmoid, bias=W["b_ffn"]).then_inc(S["sig_ffn_r"], 1)

            def norm1_out(p):
                act.wait_ge(S["xn1_T"], p + 1)
                if not first(p):
                    act.wait_ge(S["down_z1"], p)
                act.copy(xn1T[:], bank_t).then_inc(S["xn1T_r"], 1)

            def v_out(p):
                act.wait_ge(S["v_z"], p + 1)
                if not first(p):
                    act.wait_ge(S["y_z"], p)
                    act.wait_ge(S["v_split_r"], p)
                act.copy(v_twice[:].rearrange("p b k d -> p (b k d)"), bank_v).then_inc(S["v_twice_r"], 1)

            def gate_sigmoid(p):
                act.wait_ge(S["g_z"], p + 1)
                if not first(p):
                    act.wait_ge(S["g_silu_r"], p)
                act.activation(sig_g[:], bank_f[:, 0:256], ACT.Sigmoid).then_inc(S["sig_g_r"], 1)

            def shares(p):
                act.wait_ge(S["margin_r"], p + 1)
                if not first(p):
                    act.wait_ge(S["gates_r"], p)
                act.activation(share1[:], margin[:], ACT.Sigmoid).then_inc(S["share1_r"], 1)
                act.activation(share2[:], margin[:], ACT.Sigmoid, scale=-1.0).then_inc(S["share2_r"], 1)

            def qk_out(p):
                act.wait_ge(S["qk_T"], p + 1)
                if not first(p):
                    act.wait_ge(S["y_z"], p)
                act.copy(qT[:], bank_qkT[:, 0:256]).then_inc(S["qT_r"], 1)
                keys = bank_qkT[:, 256:512].rearrange("p (b k j) -> p (b k) j", b=BATCH, k=CHUNKS)
                spots = kT[:].rearrange("p b k h j -> p (b k) h j")
                act.activation(spots[:, :, 0, :], keys, ACT.Copy, scale=C["even_head"])
                act.activation(spots[:, :, 1, :], keys, ACT.Copy, scale=C["odd_head"]).then_inc(S["kT_r"], 1)

            def gates_out(p):
                act.wait_ge(S["gates_T"], p + 1)
                if not first(p):
                    act.wait_ge(S["moe_z"], p)
                    act.wait_ge(S["gate_rows_w"], p * 16)
                act.copy(gatesT[0:EXPERTS, :], bank_f[0:EXPERTS, 0:256]).then_inc(S["gatesT_r"], 1)

            def experts_relu(p):
                for c in range(DOWN):
                    if c % 2 == 0:
                        act.wait_ge(S[f"down_z{c // 2}"], p + 1)
                    if c == 0 and not first(p):
                        act.wait_ge(S["gated_h_r"], p)
                    bank = (bank_qk, bank_v)[c // 2]
                    ins = act.activation(hidden[:, c, :], bank[:, (c % 2) * 256:(c % 2) * 256 + 256], ACT.Relu,
                                         bias=V["b_down"][:, c:c + 1])
                    if c % 2:
                        ins.then_inc(S[f"hidden_r{c // 2}"], 1)

            def y_out(p):
                act.wait_ge(S["gated_y_T"], p + 1)
                if not first(p):
                    act.wait_ge(S["ret_z"], p)
                act.copy(gated_yT[:], bank_t).then_inc(S["gated_yT_r"], 1)

            def moe_sigmoid(p):
                act.wait_ge(S["moe_z"], p + 1)
                act.wait_ge(S["ret_z"], p + 1)
                if not first(p):
                    act.wait_ge(S["moe_silu_r"], p)
                act.activation(sig_moe[:], bank_dv[:, 256:512], ACT.Sigmoid, scale=0.5).then_inc(S["sig_moe_r"], 1)

            def step(s):
                a, b, c = s, s - 1, s - 2
                if live(a):
                    norm0_out(a)
                    sigmoids0(a)
                if live(b):
                    v_out(b)
                    gate_sigmoid(b)
                    shares(b)
                    qk_out(b)
                    gates_out(b)
                    experts_relu(b)
                if live(a):
                    norm1_out(a)
                if live(c):
                    y_out(c)
                    moe_sigmoid(c)

            all_steps(act, step)

        @block.vector
        def _(dve):
            spread = lambda ap, n, m: ap.rearrange("p (n o) -> p n o", o=1).to_broadcast([P, n, m])
            dve.memset(ones[:], 1.0).then_inc(S["ones_set"], 1)
            dve.memset(carry[:], 0.0).then_inc(S["carry_set"], 1)
            dve.wait_ge(S["w0_in"], 16)
            dve.tensor_reduce(abs_sum[:], W["ffn"], AX.X, ALU.add, apply_absolute_value=True).then_inc(S["abs_sum_r"], 1)
            dve.tensor_scalar(neg_b_delta[:], W["b_delta"], -1.0, None, ALU.mult).then_inc(S["neg_b_r"], 1)
            dve.wait_ge(S["abs_total"], 1)
            dve.tensor_scalar(threshold[:, 0:1], bank_f[:, 0:1], 1.0 / (DIM * DIM), 0.7, ALU.mult, ALU.mult).then_inc(S["threshold_m"], 1)
            dve.wait_ge(S["threshold_m"], 1)
            dve.tensor_scalar(threshold[:, 1:2], threshold[:, 0:1], -1.0, None, ALU.mult).then_inc(S["threshold_r"], 1)
            dve.wait_ge(S["threshold_r"], 1)
            dve.tensor_scalar(above[:], W["ffn"], threshold[:, 0:1], None, ALU.is_gt).then_inc(S["above_r"], 1)
            dve.tensor_scalar(below[:], W["ffn"], threshold[:, 1:2], None, ALU.is_lt).then_inc(S["below_r"], 1)
            dve.wait_ge(S["above_r"], 1)
            dve.wait_ge(S["below_r"], 1)
            dve.tensor_tensor(above[:], above[:], below[:], ALU.subtract).then_inc(S["tern_sign"], 1)
            dve.wait_ge(S["tern_sign"], 1)
            dve.tensor_scalar(w_tern[:], above[:], W["alpha"], None, ALU.mult).then_inc(S["tern_r"], 1)

            def statistics(p, buffer, stats, moments, n):
                for b in range(BATCH):
                    dve.wait_ge(S["x_first"], 16)
                    ins = dve.bn_stats(stats[:, b, :], pair(buffer, b, p))
                ins.then_inc(S[f"stats{n}_r"], 1)
                dve.wait_ge(S["x_first"], 16)
                dve.wait_ge(S[f"stats{n}_r"], p + 1)
                for b in range(BATCH):
                    ins = dve.bn_aggr(moments[:, b, :], stats[:, b, :])
                ins.then_inc(S[f"moments{n}_r"], 1)

            def normalise(p, buffer, moments, rstd, xn, n):
                dve.wait_ge(S[f"rstd{n}_r"], p + 1)
                dve.wait_ge(S[f"moments{n}_r"], p + 1)
                for b in range(BATCH):
                    ins = dve.tensor_scalar(xn[:, b, :], pair(buffer, b, p), moments[:, b, 0:1], rstd[:, b:b + 1],
                                            ALU.subtract, ALU.mult)
                ins.then_inc(S[f"xn{n}_r"], 1)

            def norm0_stats(p):
                if not first(p):
                    dve.wait_ge(S["x_rest"], 32)
                    dve.wait_ge(S["xn0_r"], p)
                statistics(p, x_sb, stats0, moments0, 0)

            def norm0(p):
                if not first(p):
                    dve.wait_ge(S["xn0_T"], p)
                normalise(p, x_sb, moments0, rstd0, xn0, 0)

            def recurrence(p):
                dve.wait_ge(S["delta_r"], p + 1)
                dve.wait_ge(S["keep_r"], p + 1)
                if not first(p):
                    dve.wait_ge(S["scan_r"], 2 * p)
                dve.scalar_tensor_tensor(drive[:], bank_dv[:, 256:512], W["b_value"], delta[:], ALU.add,
                                         ALU.mult).then_inc(S["drive_r"], 1)
                dve.wait_ge(S["drive_r"], p + 1)
                if first(p):
                    dve.wait_ge(S["carry_set"], 1)
                else:
                    dve.wait_ge(S["carry_r"], p)
                    dve.wait_ge(S["gated0_r"], p)
                for b in range(BATCH):
                    at = slice(b * P, (b + 1) * P)
                    dve.tensor_tensor_scan(scan[:, b, :], keep[:, at], drive[:, at], carry[:, b:b + 1],
                                           ALU.mult, ALU.add).then_inc(S["scan_r"], 1)
                dve.wait_ge(S["sig_ffn_r"], p + 1)
                dve.scalar_tensor_tensor(ffn_silu[:], bank_f[:, 0:256], W["b_ffn"], sig_ffn[:], ALU.add,
                                         ALU.mult).then_inc(S["ffn_silu_r"], 1)
                dve.wait_ge(S["scan_r"], p * 2 + 2)
                dve.tensor_copy(carry[:], scan[:, :, P - 1]).then_inc(S["carry_r"], 1)

            def residual0(p):
                dve.wait_ge(S["gated0_T"], p + 1)
                dve.tensor_tensor(both(x1_sb, p), bank_t.rearrange("p (b d) -> p b d", b=BATCH), both(x_sb, p),
                                  ALU.add).then_inc(S["x1_r"], 1)
                dve.wait_ge(S["x_first"], 16)
                if not first(p):
                    dve.wait_ge(S["xn1_r"], p)
                dve.wait_ge(S["x1_r"], p + 1)
                statistics(p, x1_sb, stats1, moments1, 1)

            def norm1(p):
                if not first(p):
                    dve.wait_ge(S["xn1_T"], p)
                normalise(p, x1_sb, moments1, rstd1, xn1, 1)

            def rotate(p):
                if first(p):
                    dve.wait_ge(S["tab_in"], 16)
                dve.wait_ge(S["qk_z"], p + 1)
                if not first(p):
                    dve.wait_ge(S["qk_r"], p)
                for i, dst in enumerate((by_cos, by_sin)):
                    t = tab[:, p, i, :] if isinstance(p, int) else tab[:, bass.ds(p, 1), i, :].rearrange("p o d -> p (o d)")
                    for b in range(BATCH):
                        ins = dve.tensor_tensor(dst[:, b, :].rearrange("p (c t) -> p c t", t=2),
                                                bank_qk[:, b * 256:b * 256 + 256].rearrange("p (c t) -> p c t", t=2),
                                                spread(t, DIM, 2), ALU.mult)
                    ins.then_inc(S[f"rot{i + 1}_r"], 1)

            def gate_silu(p):
                dve.wait_ge(S["sig_g_r"], p + 1)
                if not first(p):
                    dve.wait_ge(S["g_b_r"], p)
                dve.tensor_tensor(g_silu[:].rearrange("p b d -> p (b d)"), bank_f[:, 0:256], sig_g[:],
                                  ALU.mult).then_inc(S["g_silu_r"], 1)

            def first_largest(p, values, top, hot, n):
                dve.tensor_reduce(top[:], values[:], AX.X, ALU.max).then_inc(S[f"top{n}_r"], 1)
                dve.wait_ge(S[f"top{n}_r"], p + 1)
                dve.tensor_tensor(is_top[:], values[:], spread(top[:], BATCH, EXPERTS), ALU.is_equal).then_inc(S[f"istop{n}_r"], 1)
                dve.wait_ge(S[f"istop{n}_r"], p + 1)
                dve.tensor_tensor(is_top[:], is_top[:], C["descending"].rearrange("p (b e) -> p b e", b=BATCH),
                                  ALU.mult).then_inc(S[f"firstkey{n}_r"], 1)
                dve.wait_ge(S[f"firstkey{n}_r"], p + 1)
                dve.tensor_reduce(first_at[:], is_top[:], AX.X, ALU.max).then_inc(S[f"first{n}_r"], 1)
                dve.wait_ge(S[f"first{n}_r"], p + 1)
                dve.tensor_tensor(hot[:], is_top[:], spread(first_at[:], BATCH, EXPERTS), ALU.is_equal).then_inc(S[f"hot{n}_r"], 1)
                dve.wait_ge(S[f"hot{n}_r"], p + 1)

            def choose(p):
                dve.wait_ge(S["sig_g_r"], p + 1)
                dve.tensor_copy(logits[:].rearrange("p b e -> p (b e)"), bank_f[:, 256:272]).then_inc(S["logits_r"], 1)
                dve.wait_ge(S["logits_r"], p + 1)
                if not first(p):
                    dve.wait_ge(S["gates_r"], p)
                first_largest(p, logits, top1, hot1, 1)
                dve.scalar_tensor_tensor(rest[:], hot1[:], -3.0e38, logits[:], ALU.mult, ALU.add).then_inc(S["rest_r"], 1)
                dve.wait_ge(S["rest_r"], p + 1)
                first_largest(p, rest, top2, hot2, 2)
                dve.tensor_tensor(margin[:], top1[:], top2[:], ALU.subtract).then_inc(S["margin_r"], 1)

            def weigh(p):
                dve.wait_ge(S["share1_r"], p + 1)
                dve.wait_ge(S["share2_r"], p + 1)
                dve.tensor_tensor(hot1[:], hot1[:], spread(share1[:], BATCH, EXPERTS), ALU.mult).then_inc(S["part1_r"], 1)
                dve.tensor_tensor(hot2[:], hot2[:], spread(share2[:], BATCH, EXPERTS), ALU.mult).then_inc(S["part2_r"], 1)
                dve.wait_ge(S["part1_r"], p + 1)
                dve.wait_ge(S["part2_r"], p + 1)
                if not first(p):
                    dve.wait_ge(S["gates_T"], p)
                dve.tensor_tensor(gates[:], hot1[:], hot2[:], ALU.add).then_inc(S["gates_r"], 1)

            def gate_hidden(p):
                dve.wait_ge(S["hidden_r1"], p + 1)
                dve.wait_ge(S["gate_wide_in"], p * 32 + 32)
                if not first(p):
                    dve.wait_ge(S["moe_z"], p)
                dve.tensor_tensor(gated_h[:], hidden[:], gate_wide[:], ALU.mult).then_inc(S["gated_h_r"], 1)

            def mask_scores(p):
                if first(p):
                    dve.wait_ge(S["const_in"], 16)
                dve.wait_ge(S["scores_z"], p + 1)
                if not first(p):
                    dve.wait_ge(S["y_z"], p)
                causal = C["causal"].rearrange("p (o i) -> p o i", o=1).to_broadcast([P, BATCH * CHUNKS, CHUNK])
                for h in range(2):
                    for i in (2 * h, 2 * h + 1):
                        ins = dve.tensor_tensor(masked[:, i].rearrange("p b k i -> p (b k) i"),
                                                scores[:, i, :].rearrange("p (n i) -> p n i", i=CHUNK), causal, ALU.mult)
                    ins.then_inc(S["masked_r"], 1)

            def state_out(p, k):
                dve.wait_ge(S[f"state_k{k}"], p + 1)
                dst, done = ((state_b, "state_b_r"), (state_a, "state_a_r"))[k]
                if k == 0 and not first(p):
                    dve.wait_ge(S["y_z"], p)
                same = C["same_head"].rearrange("p (o d) -> p o d", o=1).to_broadcast([P, BATCH, DIM])
                dve.tensor_tensor(dst[:], bank_s.rearrange("p (b d) -> p b d", b=BATCH), same, ALU.mult).then_inc(S[done], 1)

            def group_centre(p):
                dve.wait_ge(S["y_z"], p + 1)
                y = bank_y.rearrange("p (g d) -> p g d", d=HEAD)
                if not first(p):
                    dve.wait_ge(S["y_norm_r"], p)
                    dve.wait_ge(S["y_sq_r"], p)
                dve.tensor_reduce(y_sum[:], y, AX.X, ALU.add).then_inc(S["y_sum_r"], 1)
                dve.wait_ge(S["y_sum_r"], p + 1)
                dve.scalar_tensor_tensor(y_mid[:], spread(y_sum[:], BATCH * HEADS, HEAD), -1.0 / HEAD, y, ALU.mult,
                                         ALU.add).then_inc(S["y_mid_r"], 1)

            def group_variance(p):
                dve.wait_ge(S["y_sq_r"], p + 1)
                if not first(p):
                    dve.wait_ge(S["y_vare_r"], p)
                dve.tensor_reduce(y_var[:], y_sq[:], AX.X, ALU.add).then_inc(S["y_var_r"], 1)

            def group_norm(p):
                dve.wait_ge(S["y_rstd_r"], p + 1)
                dve.wait_ge(S["y_mid_r"], p + 1)
                if not first(p):
                    dve.wait_ge(S["y_w_r"], p)
                dve.tensor_tensor(y_norm[:], y_mid[:], spread(y_rstd[:], BATCH * HEADS, HEAD), ALU.mult).then_inc(S["y_norm_r"], 1)

            def combine(p):
                dve.wait_ge(S["sig_moe_r"], p + 1)
                if not first(p):
                    dve.wait_ge(S["update_r"], p)
                dve.scalar_tensor_tensor(moe_silu[:], bank_dv[:, 256:512], 0.5, sig_moe[:], ALU.mult,
                                         ALU.mult).then_inc(S["moe_silu_r"], 1)
                dve.wait_ge(S["moe_silu_r"], p + 1)
                if not first(p):
                    dve.wait_ge(S["out_r"], p)
                dve.tensor_tensor(update[:].rearrange("p b d -> p (b d)"), bank_dv[:, 0:256], moe_silu[:],
                                  ALU.mult).then_inc(S["update_r"], 1)

            def step(s):
                a, b, c = s, s - 1, s - 2
                if live(a):
                    norm0_stats(a)
                    norm0(a)
                if live(c):
                    mask_scores(c)
                    state_out(c, 0)
                if live(a):
                    recurrence(a)
                if live(c):
                    state_out(c, 1)
                    group_centre(c)
                if live(b):
                    rotate(b)
                if live(a):
                    residual0(a)
                if live(b):
                    gate_silu(b)
                    choose(b)
                    weigh(b)
                if live(a):
                    norm1(a)
                if live(c):
                    group_variance(c)
                    group_norm(c)
                if live(b):
                    gate_hidden(b)
                if live(c):
                    combine(c)

            all_steps(dve, step)

        @block.gpsimd
        def _(pool):
            pool.memset(zeros[:], 0.0).then_inc(S["zeros_set"], 1)
            pool.memset(state_a[:], 0.0).then_inc(S["state_set"], 1)
            pool.memset(neg_half[:], -0.5).then_inc(S["neg_half_set"], 1)

            def inverse_root(p, moments, var, rstd, n):
                pool.wait_ge(S["neg_half_set"], 1)
                pool.wait_ge(S[f"moments{n}_r"], p + 1)
                pool.tensor_scalar(var[:], moments[:, :, 1], EPS, 1.0, ALU.add, ALU.mult).then_inc(S[f"var{n}_r"], 1)
                pool.wait_ge(S[f"var{n}_r"], p + 1)
                if not first(p):
                    pool.wait_ge(S[f"xn{n}_r"], p)
                pool.tensor_tensor(rstd[:], var[:], neg_half[:, 0:BATCH], ALU.pow).then_inc(S[f"rstd{n}_r"], 1)

            def gate0(p):
                pool.wait_ge(S["scan_r"], p * 2 + 2)
                pool.wait_ge(S["ffn_silu_r"], p + 1)
                if not first(p):
                    pool.wait_ge(S["gated0_T"], p)
                pool.tensor_tensor(gated0[:], scan[:].rearrange("p b t -> p (b t)"), ffn_silu[:], ALU.mult).then_inc(S["gated0_r"], 1)

            def rotate(p):
                pool.wait_ge(S["rot2_r"], p + 1)
                if not first(p):
                    pool.wait_ge(S["y_z"], p)
                o = qk[:].rearrange("p b i (c t) -> p (b i c) t", t=2)
                c = by_cos[:].rearrange("p b (c t) -> p (b c) t", t=2)
                n = by_sin[:].rearrange("p b (c t) -> p (b c) t", t=2)
                pool.tensor_tensor(o[:, :, 0], c[:, :, 0], n[:, :, 1], ALU.subtract)
                pool.tensor_tensor(o[:, :, 1], c[:, :, 1], n[:, :, 0], ALU.add).then_inc(S["qk_r"], 1)

            def split_v(p):
                pool.wait_ge(S["v_twice_r"], p + 1)
                if first(p):
                    pool.wait_ge(S["const_in"], 16)
                else:
                    pool.wait_ge(S["y_z"], p)
                own = C["own_heads"].rearrange("p (o d) -> p o d", o=1).to_broadcast([P, BATCH * CHUNKS, DIM])
                pool.tensor_tensor(v_split[:].rearrange("p b k d -> p (b k) d"),
                                   v_twice[:].rearrange("p b k d -> p (b k) d"), own, ALU.mult).then_inc(S["v_split_r"], 1)

            def group_square(p):
                pool.wait_ge(S["y_mid_r"], p + 1)
                if not first(p):
                    pool.wait_ge(S["y_var_r"], p)
                pool.tensor_tensor(y_sq[:], y_mid[:], y_mid[:], ALU.mult).then_inc(S["y_sq_r"], 1)

            def group_root(p):
                pool.wait_ge(S["neg_half_set"], 1)
                pool.wait_ge(S["y_var_r"], p + 1)
                pool.tensor_scalar(y_vare[:], y_var[:], 1.0 / HEAD, EPS, ALU.mult, ALU.add).then_inc(S["y_vare_r"], 1)
                pool.wait_ge(S["y_vare_r"], p + 1)
                if not first(p):
                    pool.wait_ge(S["y_norm_r"], p)
                pool.tensor_tensor(y_rstd[:], y_vare[:], neg_half[:], ALU.pow).then_inc(S["y_rstd_r"], 1)

            def group_out(p):
                pool.wait_ge(S["y_norm_r"], p + 1)
                pool.wait_ge(S["g_b_r"], p + 1)
                if not first(p):
                    pool.wait_ge(S["gated_y_r"], p)
                pool.tensor_tensor(y_w[:].rearrange("p b d -> p (b d)"), y_norm[:].rearrange("p g d -> p (g d)"),
                                   g_w[:].rearrange("p b d -> p (b d)"), ALU.mult).then_inc(S["y_w_r"], 1)
                pool.wait_ge(S["y_w_r"], p + 1)
                if not first(p):
                    pool.wait_ge(S["gated_y_T"], p)
                pool.tensor_tensor(gated_y[:].rearrange("p b d -> p (b d)"), y_w[:].rearrange("p b d -> p (b d)"),
                                   g_b[:].rearrange("p b d -> p (b d)"), ALU.add).then_inc(S["gated_y_r"], 1)

            def gate_affine(p):
                if first(p):
                    pool.wait_ge(S["w1_in"], 16)
                pool.wait_ge(S["g_silu_r"], p + 1)
                if not first(p):
                    pool.wait_ge(S["gated_y_r"], p)
                wide = lambda a: a.rearrange("p (o d) -> p o d", o=1).to_broadcast([P, BATCH, DIM])
                pool.tensor_tensor(g_w[:], g_silu[:], wide(V["gn_w"]), ALU.mult).then_inc(S["g_w_r"], 1)
                pool.tensor_tensor(g_b[:], g_silu[:], wide(V["gn_b"]), ALU.mult).then_inc(S["g_b_r"], 1)

            def residual1(p):
                pool.wait_ge(S["update_r"], p + 1)
                pool.tensor_tensor(both(out_sb, p), update[:], both(x1_sb, p), ALU.add).then_inc(S["out_r"], 1)

            def step(s):
                a, b, c = s, s - 1, s - 2
                if live(a):
                    inverse_root(a, moments0, var0, rstd0, 0)
                    gate0(a)
                if live(b):
                    rotate(b)
                    split_v(b)
                if live(a):
                    inverse_root(a, moments1, var1, rstd1, 1)
                if live(c):
                    group_square(c)
                    group_root(c)
                    group_out(c)
                if live(b):
                    gate_affine(b)
                if live(c):
                    residual1(c)

            all_steps(pool, step)


def kernel(L0_attn_seq, L0_attn_W_delta, L0_attn_b_delta, L0_attn_W_value, L0_attn_b_value, L0_ffn_weight,
           L0_ffn_alpha, L0_ffn_bias, L1_attn_W_Q, L1_attn_W_K, L1_attn_W_V, L1_attn_W_G, L1_attn_W_O,
           L1_attn_gn_weight, L1_attn_gn_bias, L1_ffn_w_gate, L1_ffn_w_noise, L1_ffn_Wd, L1_ffn_bd, L1_ffn_Wu,
           L1_ffn_bu):
    import concourse.bacc as bacc
    from concourse.bass_utils import run_bass_kernel_spmd

    heads = lambda w: np.asarray(w).transpose(1, 0, 2).reshape(DIM, DIM)
    rows = lambda v: np.broadcast_to(np.asarray(v)[None, :], (P, len(v)))
    bu = np.zeros((P, DIM), np.float32)
    bu[:EXPERTS] = L1_ffn_bu
    w0 = np.concatenate([
        np.asarray(L0_attn_W_delta).T, np.asarray(L0_attn_W_value).T, np.asarray(L0_ffn_weight).T,
        np.asarray(L0_attn_b_delta)[:, None], np.asarray(L0_attn_b_value)[:, None],
        np.asarray(L0_ffn_bias)[:, None], rows(L0_ffn_alpha)], axis=1)
    w1 = np.concatenate([
        heads(L1_attn_W_Q), heads(L1_attn_W_K), heads(L1_attn_W_V), L1_attn_W_G, L1_ffn_w_gate, L1_attn_W_O,
        np.asarray(L1_ffn_Wd).transpose(1, 0, 2).reshape(DIM, EXPERTS * NECK),
        np.asarray(L1_ffn_Wu).reshape(DOWN, P, DIM).transpose(1, 0, 2).reshape(P, DOWN * DIM),
        np.asarray(L1_ffn_bd).reshape(DOWN, P).T, bu, rows(L1_attn_gn_weight), rows(L1_attn_gn_bias)], axis=1)
    const, tables = constants()
    nc = bacc.Bacc("TRN2", target_bir_lowering=False, num_devices=1)
    arrays = {"x": np.asarray(L0_attn_seq), "w0": w0, "w1": w1, "const": const, "tables": tables}
    arrays = {k: np.ascontiguousarray(v) for k, v in arrays.items()}
    args = [nc.dram_tensor(k, v.shape, F32, kind="ExternalInput").ap() for k, v in arrays.items()]
    gate_rows = nc.dram_tensor("gate_rows", (EXPERTS, BATCH * P), F32, kind="Internal").ap()
    out = nc.dram_tensor("out", (BATCH, SEQ, DIM), F32, kind="ExternalOutput").ap()
    two_layers(nc, *args, gate_rows, out)
    r = run_bass_kernel_spmd(nc, [arrays], core_ids=[0])
    return r.results[0]["out"]
```

```python
from contextlib import ExitStack

import numpy as np
import concourse.bass as bass
from concourse import mybir

F32 = mybir.dt.float32
ALU = mybir.AluOpType
ACT = mybir.ActivationFunctionType
AX = mybir.AxisListType

P = 128
BATCH, SEQ, DIM = 2, 1024, 128
PAIRS = SEQ // P
HEADS, HEAD = 8, 16
CHUNK = 64
CHUNKS = P // CHUNK
STRIPES = 4
EXPERTS, NECK = 8, 64
DOWN = EXPERTS * NECK // P
EPS = 1e-5
LAG = 3
PEEL = 3

W_PARTS = [("delta", DIM), ("value", DIM), ("ffn", DIM), ("b_delta", 1), ("b_value", 1), ("b_ffn", 1),
           ("alpha", 1)]
V_PARTS = [("qk", 2 * DIM), ("v", DIM), ("g_logit", DIM + EXPERTS), ("o", DIM),
           ("down", EXPERTS * NECK), ("up", DOWN * DIM), ("b_down", DOWN), ("b_up", DIM),
           ("gn_w", DIM), ("gn_b", DIM)]
C_PARTS = [("identity", P), ("causal", CHUNK), ("same_head", DIM), ("even_head", 1), ("odd_head", 1), ("own_heads", DIM),
           ("descending", BATCH * EXPERTS)]


def columns(parts):
    at, out = 0, {}
    for name, n in parts:
        out[name] = (at, at + n)
        at += n
    return out, at


W_AT, W_N = columns(W_PARTS)
V_AT, V_N = columns(V_PARTS)
C_AT, C_N = columns(C_PARTS)


def constants():
    c = np.zeros((P, C_N), np.float32)
    r = np.arange(P)
    put = lambda name, a: c.__setitem__((slice(None), slice(*C_AT[name])), a)
    put("identity", np.eye(P))
    put("causal", np.arange(CHUNK)[None, :] >= (r % CHUNK)[:, None])
    put("same_head", (r // HEAD)[:, None] == (np.arange(DIM) // HEAD)[None, :])
    put("even_head", (r // HEAD % 2 == 0)[:, None])
    put("odd_head", (r // HEAD % 2 == 1)[:, None])
    put("own_heads", (r // 64)[:, None] == (np.arange(DIM) // HEAD % 2)[None, :])
    put("descending", np.tile(np.arange(EXPERTS, 0, -1), BATCH)[None, :])
    f = np.float32
    half = HEAD // 2
    scale = (np.arange(0, HEAD, 2, dtype=f) + f(0.4 * HEAD)) / f(1.4 * HEAD)
    gamma = (1.0 - np.exp(np.linspace(np.log(1 / 32), np.log(1 / 64), HEADS))).astype(f)
    pos = np.arange(SEQ, dtype=f)
    freq = (f(1.0) / f(10000.0) ** (np.arange(half, dtype=f) / f(half))).astype(f)
    angle = (pos[:, None] * freq[None, :]).astype(f).astype(np.float64)
    mid = pos.astype(np.float64) - SEQ // 2
    grow = (scale.astype(np.float64)[None, None, :] ** (mid[:, None, None] / 64.0)
            * gamma.astype(np.float64)[None, :, None] ** mid[:, None, None])
    both = np.stack([grow, 1.0 / grow], 1)
    tables = np.stack([both * np.cos(angle)[:, None, None, :], both * np.sin(angle)[:, None, None, :]], 1)
    tables = tables.reshape(PAIRS, P, 2, DIM).transpose(1, 0, 2, 3)
    return c, np.ascontiguousarray(tables.astype(f))


def two_layers(nc, x, w0, w1, const, tables, gate_rows, out):
    with ExitStack() as ctx:
        def sb(name, *shape):
            return ctx.enter_context(nc.sbuf_tensor(name, [P, *shape], F32))

        def sem(name):
            return ctx.enter_context(nc.semaphore(name))

        x_sb = sb("x_sb", BATCH, PAIRS, DIM)
        x1_sb = sb("x1_sb", BATCH, PAIRS, DIM)
        out_sb = sb("out_sb", BATCH, PAIRS, DIM)
        tab = sb("tab", PAIRS, 2, DIM)
        w0_sb = sb("w0_sb", W_N)
        w1_sb = sb("w1_sb", V_N)
        c_sb = sb("c_sb", C_N)
        W = {k: w0_sb[:, a:b] for k, (a, b) in W_AT.items()}
        V = {k: w1_sb[:, a:b] for k, (a, b) in V_AT.items()}
        C = {k: c_sb[:, a:b] for k, (a, b) in C_AT.items()}
        abs_sum = sb("abs_sum", 1)
        ones = sb("ones", P)
        zeros = sb("zeros", BATCH * DIM)
        threshold = sb("threshold", 2)
        above = sb("above", DIM)
        below = sb("below", DIM)
        w_tern = sb("w_tern", DIM)
        neg_b_delta = sb("neg_b_delta", 1)
        neg_half = sb("neg_half", BATCH * HEADS)
        stats0 = sb("stats0", BATCH, 6)
        moments0 = sb("moments0", BATCH, 2)
        var0 = sb("var0", BATCH)
        rstd0 = sb("rstd0", BATCH)
        xn0 = sb("xn0", BATCH, DIM)
        xn0T = sb("xn0T", BATCH * P)
        keep = sb("keep", BATCH * P)
        delta = sb("delta", BATCH * P)
        sig_ffn = sb("sig_ffn", BATCH * P)
        drive = sb("drive", BATCH * P)
        carry = sb("carry", BATCH)
        scan = sb("scan", BATCH, P)
        ffn_silu = sb("ffn_silu", BATCH * P)
        gated0 = sb("gated0", BATCH * P)
        stats1 = sb("stats1", BATCH, 6)
        moments1 = sb("moments1", BATCH, 2)
        var1 = sb("var1", BATCH)
        rstd1 = sb("rstd1", BATCH)
        xn1 = sb("xn1", BATCH, DIM)
        xn1T = sb("xn1T", BATCH * P)
        xn1T_twice = sb("xn1T_twice", BATCH * CHUNKS, 2, CHUNK)
        by_cos = sb("by_cos", BATCH, 2 * DIM)
        by_sin = sb("by_sin", BATCH, 2 * DIM)
        qk = sb("qk", BATCH, 2, DIM)
        v_twice = sb("v_twice", BATCH, CHUNKS, DIM)
        v_split = sb("v_split", BATCH, CHUNKS, DIM)
        qT = sb("qT", BATCH * P)
        kT = sb("kT", BATCH, CHUNKS, 2, CHUNK)
        sig_g = sb("sig_g", BATCH, DIM)
        g_silu = sb("g_silu", BATCH, DIM)
        g_w = sb("g_w", BATCH, DIM)
        g_b = sb("g_b", BATCH, DIM)
        logits = sb("logits", BATCH, EXPERTS)
        top1 = sb("top1", BATCH)
        top2 = sb("top2", BATCH)
        is_top = sb("is_top", BATCH, EXPERTS)
        first_at = sb("first_at", BATCH)
        hot1 = sb("hot1", BATCH, EXPERTS)
        rest = sb("rest", BATCH, EXPERTS)
        hot2 = sb("hot2", BATCH, EXPERTS)
        margin = sb("margin", BATCH)
        share1 = sb("share1", BATCH)
        share2 = sb("share2", BATCH)
        gates = sb("gates", BATCH, EXPERTS)
        gatesT = sb("gatesT", BATCH * P)
        gate_wide = sb("gate_wide", DOWN, BATCH * P)
        hidden = sb("hidden", DOWN, BATCH * P)
        gated_h = sb("gated_h", DOWN, BATCH * P)
        masked = sb("masked", STRIPES, BATCH, CHUNKS, CHUNK)
        state_a = sb("state_a", BATCH, DIM)
        state_b = sb("state_b", BATCH, DIM)
        y_sum = sb("y_sum", BATCH * HEADS)
        y_mid = sb("y_mid", BATCH * HEADS, HEAD)
        y_sq = sb("y_sq", BATCH * HEADS, HEAD)
        y_var = sb("y_var", BATCH * HEADS)
        y_vare = sb("y_vare", BATCH * HEADS)
        y_rstd = sb("y_rstd", BATCH * HEADS)
        y_norm = sb("y_norm", BATCH * HEADS, HEAD)
        y_w = sb("y_w", BATCH, DIM)
        gated_y = sb("gated_y", BATCH, DIM)
        gated_yT = sb("gated_yT", BATCH * P)
        sig_moe = sb("sig_moe", BATCH * DIM)
        moe_silu = sb("moe_silu", BATCH * DIM)
        update = sb("update", BATCH, DIM)

        ps = ctx.enter_context(nc.psum_tensor("ps", [P, 8, 512], F32))
        bank_t = ps[:, 0, 0:256]
        bank_x = ps[:, 0, 256:512]
        bank_dv = ps[:, 1, :]
        bank_f = ps[:, 2, :]
        g_logits = bank_f[:, 0:BATCH * (DIM + EXPERTS)].rearrange("p (b n) -> p b n", b=BATCH)
        bank_qk = ps[:, 3, :]
        bank_v = ps[:, 4, :]
        bank_qkT = ps[:, 5, :]
        bank_y = ps[:, 6, 0:256]
        bank_s = ps[:, 7, 0:256]
        scores = ps[:, 3:7, 0:256]

        names = """x_first x_rest w0_in w1_in const_in tab_in ones_set zeros_set carry_set state_set
            neg_half_set abs_sum_r abs_total threshold_m threshold_r above_r below_r tern_sign tern_r neg_b_r
            stats0_r moments0_r var0_r rstd0_r xn0_r xn0_T xn0T_r dv_z ffn_z keep_r delta_r sig_ffn_r drive_r
            scan_r carry_r ffn_silu_r gated0_r gated0_T x1_r stats1_r moments1_r var1_r rstd1_r xn1_r xn1_T
            xn1T_r xn1T_twice_r qk_z v_z g_z rot1_r rot2_r qk_r v_twice_r v_split_r qk_T qT_r kT_r sig_g_r g_silu_r g_w_r
            g_b_r logits_r top1_r istop1_r firstkey1_r first1_r hot1_r rest_r top2_r istop2_r firstkey2_r
            first2_r hot2_r margin_r share1_r share2_r part1_r part2_r gates_r gates_T gatesT_r gate_rows_w
            gate_wide_in down_z0 down_z1 hidden_r0 hidden_r1 gated_h_r moe_z scores_z masked_r state_k0
            state_b_r state_k1 state_a_r y_z y_sum_r y_mid_r y_sq_r y_var_r y_vare_r y_rstd_r y_norm_r y_w_r
            gated_y_r gated_y_T gated_yT_r ret_z sig_moe_r moe_silu_r update_r out_r out_w""".split()
        S = {n: sem(n) for n in names}

        def live(p):
            return not isinstance(p, int) or 0 <= p < PAIRS

        def first(p):
            return isinstance(p, int) and p == 0

        def at_least(p, n):
            return not isinstance(p, int) or p >= n

        def through(p):
            return min(p + 1, PAIRS) if isinstance(p, int) else p + 1

        def all_steps(engine, step):
            for s in range(-1, PEEL):
                step(s)
            with engine.Fori(PEEL + 2, PAIRS + 1) as count:
                step(count - 2)
            for s in range(PAIRS - 1, PAIRS + LAG):
                step(s)

        def pair(buffer, b, p):
            return buffer[:, b, p, :] if isinstance(p, int) else buffer[:, b, bass.ds(p, 1), :]

        def both(buffer, p):
            return buffer[:, :, p, :] if isinstance(p, int) else buffer[:, :, bass.ds(p, 1), :]

        block = ctx.enter_context(nc.Block())

        @block.sync
        def _(sp):
            x_in = x.rearrange("b (p t) d -> t b p d", t=P)
            sp.dma_start(x_sb[:, :, 0:1, :], x_in[:, :, 0:1, :]).then_inc(S["x_first"], 16)
            sp.dma_start(w0_sb[:], w0).then_inc(S["w0_in"], 16)
            sp.dma_start(x_sb[:, 0, 1:PAIRS, :], x_in[:, 0, 1:PAIRS, :]).then_inc(S["x_rest"], 16)
            sp.dma_start(x_sb[:, 1, 1:PAIRS, :], x_in[:, 1, 1:PAIRS, :]).then_inc(S["x_rest"], 16)
            sp.dma_start(w1_sb[:], w1).then_inc(S["w1_in"], 16)
            sp.dma_start(tab[:], tables).then_inc(S["tab_in"], 16)

            def spread_gates(p):
                sp.wait_ge(S["gatesT_r"], p + 1)
                if not first(p):
                    sp.wait_ge(S["gate_wide_in"], p * 32)
                sp.dma_start(gate_rows, gatesT[0:EXPERTS, :]).then_inc(S["gate_rows_w"], 16)
                sp.wait_ge(S["gate_rows_w"], p * 16 + 16)
                if not first(p):
                    sp.wait_ge(S["gated_h_r"], p)
                rows = gate_rows.rearrange("(c h) t -> h c t", h=2)
                for h in range(2):
                    src = rows[h].rearrange("(o c) t -> o c t", o=1).to_broadcast([NECK, DOWN, BATCH * P])
                    sp.dma_start(gate_wide[NECK * h:NECK * (h + 1)], src).then_inc(S["gate_wide_in"], 16)

            def store(p):
                sp.wait_ge(S["out_r"], p + 1)
                o = out.rearrange("b (p t) d -> t b p d", t=P)
                for b in range(BATCH):
                    if isinstance(p, int):
                        dst = o[:, b, p, :]
                    else:
                        dst = o[:, b, bass.ds(p, 1), :]
                    sp.dma_start(dst, pair(out_sb, b, p)).then_inc(S["out_w"], 16)

            def step(s):
                if live(s - 2):
                    spread_gates(s - 2)
                if live(s - 3):
                    store(s - 3)

            all_steps(sp, step)
            sp.wait_ge(S["out_w"], 16 * BATCH * PAIRS)

        @block.tensor
        def _(pe):
            half = lambda b: slice(b * P, (b + 1) * P)
            pe.wait_ge(S["ones_set"], 1)
            pe.wait_ge(S["abs_sum_r"], 1)
            pe.matmul(bank_f[:, 0:1], ones[:], abs_sum[:], start=True, stop=True).then_inc(S["abs_total"], 1)
            pe.wait_ge(S["zeros_set"], 1)
            pe.matmul(bank_s, zeros[:, 0:P], zeros[:], start=True, stop=False, skip_group_check=True)
            pe.wait_ge(S["const_in"], 16)

            def turn_y(p):
                pe.wait_ge(S["gated_y_r"], p + 1)
                pe.wait_ge(S["xn1T_r"], through(p + 2))
                pe.wait_ge(S["xn0T_r"], through(p + 3))
                if isinstance(p, int) and p > 0:
                    pe.wait_ge(S["update_r"], p)
                for b in range(BATCH):
                    mm = pe.transpose(bank_t[:, half(b)], gated_y[:, b, :], C["identity"])
                mm.then_inc(S["gated_y_T"], 1)

            def turn_x(p):
                pe.wait_ge(S["xn0_r"], p + 1)
                if at_least(p, 2):
                    pe.wait_ge(S["xn1T_r"], p - 1)
                if at_least(p, 4):
                    pe.wait_ge(S["update_r"], p - 3)
                for b in range(BATCH):
                    mm = pe.transpose(bank_x[:, half(b)], xn0[:, b, :], C["identity"])
                mm.then_inc(S["xn0_T"], 1)

            def output(p):
                pe.wait_ge(S["gated_yT_r"], p + 1)
                for b in range(BATCH):
                    mm = pe.matmul(bank_t[:, half(b)], gated_yT[:, half(b)], V["o"], start=True, stop=True)
                mm.then_inc(S["ret_z"], 1)

            def project0(p):
                pe.wait_ge(S["xn0T_r"], p + 1)
                if first(p):
                    pe.wait_ge(S["w0_in"], 16)
                if not first(p):
                    pe.wait_ge(S["x1_r"], p)
                if at_least(p, 3):
                    pe.wait_ge(S["moe_silu_r"], p - 2)
                pe.matmul(bank_dv[:, 0:256], W["delta"], xn0T[:], start=True, stop=True)
                pe.matmul(bank_dv[:, 256:512], W["value"], xn0T[:], start=True, stop=True).then_inc(S["dv_z"], 1)
                if first(p):
                    pe.wait_ge(S["tern_r"], 1)
                if at_least(p, 2):
                    pe.wait_ge(S["g_silu_r"], p - 1)
                    pe.wait_ge(S["logits_r"], p - 1)
                pe.matmul(bank_f[:, 0:256], w_tern[:], xn0T[:], start=True, stop=True).then_inc(S["ffn_z"], 1)

            def turn_gated0(p):
                pe.wait_ge(S["gated0_r"], p + 1)
                for b in range(BATCH):
                    mm = pe.transpose(bank_dv[:, half(b)], gated0[:, half(b)], C["identity"])
                mm.then_inc(S["gated0_T"], 1)

            def turn_x1(p):
                pe.wait_ge(S["xn1_r"], p + 1)
                pe.wait_ge(S["xn0T_r"], through(p + 1))
                if at_least(p, 3):
                    pe.wait_ge(S["update_r"], p - 2)
                for b in range(BATCH):
                    mm = pe.transpose(bank_t[:, half(b)], xn1[:, b, :], C["identity"])
                mm.then_inc(S["xn1_T"], 1)

            def project1(p):
                if first(p):
                    pe.wait_ge(S["w1_in"], 16)
                pe.wait_ge(S["xn1T_r"], p + 1)
                if not first(p):
                    pe.wait_ge(S["hidden_r1"], p)
                    pe.wait_ge(S["masked_r"], 2 * p)
                for b in range(BATCH):
                    mm = pe.matmul(bank_qk[:, b * 256:b * 256 + 256], xn1T[:, half(b)], V["qk"],
                                   start=True, stop=True)
                mm.then_inc(S["qk_z"], 1)
                pe.wait_ge(S["xn1T_twice_r"], p + 1)
                for b in range(BATCH):
                    for k in range(CHUNKS):
                        n = b * CHUNKS + k
                        mm = pe.matmul(bank_v[:, n * DIM:(n + 1) * DIM], xn1T_twice[:, n, :, :].rearrange("p h t -> p (h t)"),
                                       V["v"], start=True, stop=True)
                mm.then_inc(S["v_z"], 1)
                pe.wait_ge(S["ffn_silu_r"], through(p + 1))
                if not first(p):
                    pe.wait_ge(S["gatesT_r"], p)
                for b in range(BATCH):
                    mm = pe.matmul(g_logits[:, b, :], xn1T[:, half(b)], V["g_logit"], start=True, stop=True)
                mm.then_inc(S["g_z"], 1)

            def turn_qk(p):
                pe.wait_ge(S["qk_r"], p + 1)
                for i in range(2):
                    for b in range(BATCH):
                        mm = pe.transpose(bank_qkT[:, (2 * i + b) * P:(2 * i + b + 1) * P], qk[:, b, i, :],
                                          C["identity"])
                mm.then_inc(S["qk_T"], 1)

            def experts_down(p):
                pe.wait_ge(S["rot2_r"], p + 1)
                for c in range(DOWN):
                    if c == 2:
                        pe.wait_ge(S["v_twice_r"], p + 1)
                    bank = (bank_qk, bank_v)[c // 2]
                    mm = pe.matmul(bank[:, (c % 2) * 256:(c % 2) * 256 + 256], V["down"][:, c * P:(c + 1) * P],
                                   xn1T[:], start=True, stop=True)
                    if c % 2:
                        mm.then_inc(S[f"down_z{c // 2}"], 1)

            def turn_gates(p):
                pe.wait_ge(S["gates_r"], p + 1)
                pe.wait_ge(S["g_silu_r"], p + 1)
                pe.wait_ge(S["ffn_silu_r"], through(p + 2))
                for b in range(BATCH):
                    mm = pe.transpose(bank_f[0:EXPERTS, half(b)], gates[:, b, :], C["identity"])
                mm.then_inc(S["gates_T"], 1)

            def score(p):
                pe.wait_ge(S["qT_r"], p + 1)
                pe.wait_ge(S["kT_r"], p + 1)
                pe.wait_ge(S["hidden_r1"], p + 1)
                if not first(p):
                    pe.wait_ge(S["y_mid_r"], p)
                for b in range(BATCH):
                    for k in range(CHUNKS):
                        for i in range(STRIPES):
                            rows = slice(32 * i, 32 * i + 32)
                            at = b * P + k * CHUNK
                            mm = pe.matmul(scores[:, i, at:at + CHUNK], kT[rows, b, k, :, :], qT[rows, at:at + CHUNK],
                                           start=True, stop=True, tile_position=(32 * i, 0))
                mm.then_inc(S["scores_z"], 1)

            def add_to_state(p, k):
                rows = slice(64 * k, 64 * k + 64)
                if k == 0:
                    pe.wait_ge(S["v_twice_r"], p + 1)
                    if first(p):
                        pe.wait_ge(S["state_set"], 1)
                    else:
                        pe.wait_ge(S["state_a_r"], p)
                else:
                    pe.wait_ge(S["state_b_r"], p + 1)
                for b in range(BATCH):
                    mm = pe.matmul(bank_s[:, b * DIM:(b + 1) * DIM], qk[rows, b, 1, :], v_twice[rows, b, k, :],
                                   start=False, stop=False, skip_group_check=True, tile_position=(64 * k, 0))
                mm.then_inc(S[f"state_k{k}"], 1)

            def retain(p):
                def read_out(k):
                    rows = slice(64 * k, 64 * k + 64)
                    state = (state_a, state_b)[k]
                    for b in range(BATCH):
                        at = b * P + k * CHUNK
                        pe.matmul(bank_y[rows, b * DIM:(b + 1) * DIM], qT[:, at:at + CHUNK], state[:, b, :],
                                  start=True, stop=False, skip_group_check=True)
                        for i in range(STRIPES):
                            mm = pe.matmul(bank_y[rows, b * DIM + 32 * i:b * DIM + 32 * i + 32],
                                           masked[:, i, b, k, :], v_split[:, b, k, 32 * i:32 * i + 32],
                                           start=False, stop=(i == STRIPES - 1), skip_group_check=True)
                    return mm

                pe.wait_ge(S["masked_r"], 2 * p + 2)
                pe.wait_ge(S["v_split_r"], p + 1)
                read_out(0)
                add_to_state(p, 1)
                read_out(1).then_inc(S["y_z"], 1)

            def experts_up(p):
                pe.wait_ge(S["gated_h_r"], p + 1)
                pe.wait_ge(S["x1_r"], through(p + 2))
                for b in range(BATCH):
                    o = bank_dv[:, 256 + b * DIM:256 + (b + 1) * DIM]
                    for c in range(DOWN):
                        pe.matmul(o, gated_h[:, c, half(b)], V["up"][:, c * DIM:(c + 1) * DIM],
                                  start=(c == 0), stop=False)
                    mm = pe.matmul(o, gatesT[0:EXPERTS, half(b)], V["b_up"][0:EXPERTS, :], start=False, stop=True)
                mm.then_inc(S["moe_z"], 1)

            def step(s):
                z, a, b, c, d = s + 1, s, s - 1, s - 2, s - 3
                if live(a):
                    project0(a)
                if live(c):
                    score(c)
                    turn_gates(c)
                if live(d):
                    turn_y(d)
                if live(a):
                    turn_gated0(a)
                if live(c):
                    add_to_state(c, 0)
                if live(d):
                    output(d)
                if live(c):
                    retain(c)
                if live(b):
                    project1(b)
                if live(z):
                    turn_x(z)
                if live(c):
                    experts_up(c)
                if live(b):
                    experts_down(b)
                    turn_qk(b)
                if live(a):
                    turn_x1(a)

            all_steps(pe, step)

        @block.scalar
        def _(act):
            act.dma_start(c_sb[:], const).then_inc(S["const_in"], 16)

            def norm0_out(p):
                act.wait_ge(S["xn0_T"], p + 1)
                if not first(p):
                    act.wait_ge(S["ffn_z"], p)
                act.copy(xn0T[:], bank_x).then_inc(S["xn0T_r"], 1)

            def sigmoids0(p):
                if first(p):
                    act.wait_ge(S["w0_in"], 16)
                    act.wait_ge(S["neg_b_r"], 1)
                act.wait_ge(S["dv_z"], p + 1)
                if not first(p):
                    act.wait_ge(S["drive_r"], p)
                act.activation(delta[:], bank_dv[:, 0:256], ACT.Sigmoid, bias=W["b_delta"]).then_inc(S["delta_r"], 1)
                if not first(p):
                    act.wait_ge(S["scan_r"], 2 * p)
                act.activation(keep[:], bank_dv[:, 0:256], ACT.Sigmoid, bias=neg_b_delta[:], scale=-1.0).then_inc(S["keep_r"], 1)
                act.wait_ge(S["ffn_z"], p + 1)
                if not first(p):
                    act.wait_ge(S["ffn_silu_r"], p)
                act.activation(sig_ffn[:], bank_f[:, 0:256], ACT.Sigmoid, bias=W["b_ffn"]).then_inc(S["sig_ffn_r"], 1)

            def norm1_out(p):
                act.wait_ge(S["xn1_T"], p + 1)
                if not first(p):
                    act.wait_ge(S["down_z1"], p)
                chunks = bank_t.rearrange("p (n o t) -> p n o t", o=1, t=CHUNK).to_broadcast([P, BATCH * CHUNKS, 2, CHUNK])
                act.copy(xn1T_twice[:], chunks).then_inc(S["xn1T_twice_r"], 1)
                act.copy(xn1T[:], bank_t).then_inc(S["xn1T_r"], 1)

            def v_out(p):
                act.wait_ge(S["v_z"], p + 1)
                if not first(p):
                    act.wait_ge(S["y_z"], p)
                    act.wait_ge(S["v_split_r"], p)
                act.copy(v_twice[:].rearrange("p b k d -> p (b k d)"), bank_v).then_inc(S["v_twice_r"], 1)

            def gate_sigmoid(p):
                act.wait_ge(S["g_z"], p + 1)
                if not first(p):
                    act.wait_ge(S["g_silu_r"], p)
                act.activation(sig_g[:], g_logits[:, :, 0:DIM], ACT.Sigmoid).then_inc(S["sig_g_r"], 1)

            def shares(p):
                act.wait_ge(S["margin_r"], p + 1)
                if not first(p):
                    act.wait_ge(S["gates_r"], p)
                act.activation(share1[:], margin[:], ACT.Sigmoid).then_inc(S["share1_r"], 1)
                act.activation(share2[:], margin[:], ACT.Sigmoid, scale=-1.0).then_inc(S["share2_r"], 1)

            def qk_out(p):
                act.wait_ge(S["qk_T"], p + 1)
                if not first(p):
                    act.wait_ge(S["y_z"], p)
                act.copy(qT[:], bank_qkT[:, 0:256]).then_inc(S["qT_r"], 1)
                keys = bank_qkT[:, 256:512].rearrange("p (b k j) -> p (b k) j", b=BATCH, k=CHUNKS)
                spots = kT[:].rearrange("p b k h j -> p (b k) h j")
                act.activation(spots[:, :, 0, :], keys, ACT.Copy, scale=C["even_head"])
                act.activation(spots[:, :, 1, :], keys, ACT.Copy, scale=C["odd_head"]).then_inc(S["kT_r"], 1)

            def gates_out(p):
                act.wait_ge(S["gates_T"], p + 1)
                if not first(p):
                    act.wait_ge(S["moe_z"], p)
                    act.wait_ge(S["gate_rows_w"], p * 16)
                act.copy(gatesT[0:EXPERTS, :], bank_f[0:EXPERTS, 0:256]).then_inc(S["gatesT_r"], 1)

            def experts_relu(p):
                for c in range(DOWN):
                    if c % 2 == 0:
                        act.wait_ge(S[f"down_z{c // 2}"], p + 1)
                    if c == 0 and not first(p):
                        act.wait_ge(S["gated_h_r"], p)
                    bank = (bank_qk, bank_v)[c // 2]
                    ins = act.activation(hidden[:, c, :], bank[:, (c % 2) * 256:(c % 2) * 256 + 256], ACT.Relu,
                                         bias=V["b_down"][:, c:c + 1])
                    if c % 2:
                        ins.then_inc(S[f"hidden_r{c // 2}"], 1)

            def y_out(p):
                act.wait_ge(S["gated_y_T"], p + 1)
                act.wait_ge(S["moe_z"], p + 1)
                act.copy(gated_yT[:], bank_t).then_inc(S["gated_yT_r"], 1)

            def moe_sigmoid(p):
                act.wait_ge(S["moe_z"], p + 1)
                if not first(p):
                    act.wait_ge(S["moe_silu_r"], p)
                act.activation(sig_moe[:], bank_dv[:, 256:512], ACT.Sigmoid, scale=0.5).then_inc(S["sig_moe_r"], 1)

            def step(s):
                z, a, b, c, d = s + 1, s, s - 1, s - 2, s - 3
                if live(a):
                    sigmoids0(a)
                if live(b):
                    norm1_out(b)
                if live(c):
                    gates_out(c)
                if live(d):
                    y_out(d)
                if live(b):
                    v_out(b)
                    gate_sigmoid(b)
                if live(z):
                    norm0_out(z)
                if live(c):
                    moe_sigmoid(c)
                if live(b):
                    experts_relu(b)
                    qk_out(b)
                    shares(b)

            all_steps(act, step)

        @block.vector
        def _(dve):
            spread = lambda ap, n, m: ap.rearrange("p (n o) -> p n o", o=1).to_broadcast([P, n, m])
            dve.memset(ones[:], 1.0).then_inc(S["ones_set"], 1)
            dve.memset(carry[:], 0.0).then_inc(S["carry_set"], 1)
            dve.wait_ge(S["w0_in"], 16)
            dve.tensor_reduce(abs_sum[:], W["ffn"], AX.X, ALU.add, apply_absolute_value=True).then_inc(S["abs_sum_r"], 1)
            dve.tensor_scalar(neg_b_delta[:], W["b_delta"], -1.0, None, ALU.mult).then_inc(S["neg_b_r"], 1)
            dve.wait_ge(S["abs_total"], 1)
            dve.tensor_scalar(threshold[:, 0:1], bank_f[:, 0:1], 1.0 / (DIM * DIM), 0.7, ALU.mult, ALU.mult).then_inc(S["threshold_m"], 1)
            dve.wait_ge(S["threshold_m"], 1)
            dve.tensor_scalar(threshold[:, 1:2], threshold[:, 0:1], -1.0, None, ALU.mult).then_inc(S["threshold_r"], 1)
            dve.wait_ge(S["threshold_r"], 1)
            dve.tensor_scalar(above[:], W["ffn"], threshold[:, 0:1], None, ALU.is_gt).then_inc(S["above_r"], 1)
            dve.tensor_scalar(below[:], W["ffn"], threshold[:, 1:2], None, ALU.is_lt).then_inc(S["below_r"], 1)
            dve.wait_ge(S["above_r"], 1)
            dve.wait_ge(S["below_r"], 1)
            dve.tensor_tensor(above[:], above[:], below[:], ALU.subtract).then_inc(S["tern_sign"], 1)
            dve.wait_ge(S["tern_sign"], 1)
            dve.tensor_scalar(w_tern[:], above[:], W["alpha"], None, ALU.mult).then_inc(S["tern_r"], 1)

            def statistics(p, buffer, stats, moments, n):
                for b in range(BATCH):
                    dve.wait_ge(S["x_first"], 16)
                    ins = dve.bn_stats(stats[:, b, :], pair(buffer, b, p))
                ins.then_inc(S[f"stats{n}_r"], 1)
                dve.wait_ge(S["x_first"], 16)
                dve.wait_ge(S[f"stats{n}_r"], p + 1)
                for b in range(BATCH):
                    ins = dve.bn_aggr(moments[:, b, :], stats[:, b, :])
                ins.then_inc(S[f"moments{n}_r"], 1)

            def normalise(p, buffer, moments, rstd, xn, n):
                dve.wait_ge(S[f"rstd{n}_r"], p + 1)
                dve.wait_ge(S[f"moments{n}_r"], p + 1)
                for b in range(BATCH):
                    ins = dve.tensor_scalar(xn[:, b, :], pair(buffer, b, p), moments[:, b, 0:1], rstd[:, b:b + 1],
                                            ALU.subtract, ALU.mult)
                ins.then_inc(S[f"xn{n}_r"], 1)

            def norm0_stats(p):
                if not first(p):
                    dve.wait_ge(S["x_rest"], 32)
                    dve.wait_ge(S["xn0_r"], p)
                statistics(p, x_sb, stats0, moments0, 0)

            def norm0(p):
                if not first(p):
                    dve.wait_ge(S["xn0_T"], p)
                normalise(p, x_sb, moments0, rstd0, xn0, 0)

            def recurrence(p):
                dve.wait_ge(S["delta_r"], p + 1)
                dve.wait_ge(S["keep_r"], p + 1)
                if not first(p):
                    dve.wait_ge(S["scan_r"], 2 * p)
                dve.scalar_tensor_tensor(drive[:], bank_dv[:, 256:512], W["b_value"], delta[:], ALU.add,
                                         ALU.mult).then_inc(S["drive_r"], 1)
                dve.wait_ge(S["drive_r"], p + 1)
                if first(p):
                    dve.wait_ge(S["carry_set"], 1)
                else:
                    dve.wait_ge(S["carry_r"], p)
                    dve.wait_ge(S["gated0_r"], p)
                for b in range(BATCH):
                    at = slice(b * P, (b + 1) * P)
                    dve.tensor_tensor_scan(scan[:, b, :], keep[:, at], drive[:, at], carry[:, b:b + 1],
                                           ALU.mult, ALU.add).then_inc(S["scan_r"], 1)
                dve.wait_ge(S["sig_ffn_r"], p + 1)
                dve.scalar_tensor_tensor(ffn_silu[:], bank_f[:, 0:256], W["b_ffn"], sig_ffn[:], ALU.add,
                                         ALU.mult).then_inc(S["ffn_silu_r"], 1)
                dve.wait_ge(S["scan_r"], p * 2 + 2)
                dve.tensor_copy(carry[:], scan[:, :, P - 1]).then_inc(S["carry_r"], 1)

            def residual0(p):
                dve.wait_ge(S["gated0_T"], p + 1)
                dve.tensor_tensor(both(x1_sb, p), bank_dv[:, 0:256].rearrange("p (b d) -> p b d", b=BATCH), both(x_sb, p),
                                  ALU.add).then_inc(S["x1_r"], 1)
                dve.wait_ge(S["x_first"], 16)
                if not first(p):
                    dve.wait_ge(S["xn1_r"], p)
                dve.wait_ge(S["x1_r"], p + 1)
                statistics(p, x1_sb, stats1, moments1, 1)

            def norm1(p):
                if not first(p):
                    dve.wait_ge(S["xn1_T"], p)
                normalise(p, x1_sb, moments1, rstd1, xn1, 1)

            def rotate(p):
                if first(p):
                    dve.wait_ge(S["tab_in"], 16)
                dve.wait_ge(S["qk_z"], p + 1)
                if not first(p):
                    dve.wait_ge(S["qk_r"], p)
                for i, dst in enumerate((by_cos, by_sin)):
                    t = tab[:, p, i, :] if isinstance(p, int) else tab[:, bass.ds(p, 1), i, :].rearrange("p o d -> p (o d)")
                    for b in range(BATCH):
                        ins = dve.tensor_tensor(dst[:, b, :].rearrange("p (c t) -> p c t", t=2),
                                                bank_qk[:, b * 256:b * 256 + 256].rearrange("p (c t) -> p c t", t=2),
                                                spread(t, DIM, 2), ALU.mult)
                    ins.then_inc(S[f"rot{i + 1}_r"], 1)

            def gate_silu(p):
                dve.wait_ge(S["sig_g_r"], p + 1)
                if not first(p):
                    dve.wait_ge(S["g_b_r"], p)
                dve.tensor_tensor(g_silu[:], g_logits[:, :, 0:DIM], sig_g[:], ALU.mult).then_inc(S["g_silu_r"], 1)

            def first_largest(p, values, top, hot, n):
                dve.tensor_reduce(top[:], values[:], AX.X, ALU.max).then_inc(S[f"top{n}_r"], 1)
                dve.wait_ge(S[f"top{n}_r"], p + 1)
                dve.tensor_tensor(is_top[:], values[:], spread(top[:], BATCH, EXPERTS), ALU.is_equal).then_inc(S[f"istop{n}_r"], 1)
                dve.wait_ge(S[f"istop{n}_r"], p + 1)
                dve.tensor_tensor(is_top[:], is_top[:], C["descending"].rearrange("p (b e) -> p b e", b=BATCH),
                                  ALU.mult).then_inc(S[f"firstkey{n}_r"], 1)
                dve.wait_ge(S[f"firstkey{n}_r"], p + 1)
                dve.tensor_reduce(first_at[:], is_top[:], AX.X, ALU.max).then_inc(S[f"first{n}_r"], 1)
                dve.wait_ge(S[f"first{n}_r"], p + 1)
                dve.tensor_tensor(hot[:], is_top[:], spread(first_at[:], BATCH, EXPERTS), ALU.is_equal).then_inc(S[f"hot{n}_r"], 1)
                dve.wait_ge(S[f"hot{n}_r"], p + 1)

            def choose_first(p):
                dve.wait_ge(S["sig_g_r"], p + 1)
                dve.tensor_copy(logits[:], g_logits[:, :, DIM:]).then_inc(S["logits_r"], 1)
                dve.wait_ge(S["logits_r"], p + 1)
                if not first(p):
                    dve.wait_ge(S["gates_r"], p)
                first_largest(p, logits, top1, hot1, 1)
                dve.scalar_tensor_tensor(rest[:], hot1[:], -3.0e38, logits[:], ALU.mult, ALU.add).then_inc(S["rest_r"], 1)

            def choose_second(p):
                dve.wait_ge(S["rest_r"], p + 1)
                first_largest(p, rest, top2, hot2, 2)
                dve.tensor_tensor(margin[:], top1[:], top2[:], ALU.subtract).then_inc(S["margin_r"], 1)

            def weigh(p):
                dve.wait_ge(S["share1_r"], p + 1)
                dve.wait_ge(S["share2_r"], p + 1)
                dve.tensor_tensor(hot1[:], hot1[:], spread(share1[:], BATCH, EXPERTS), ALU.mult).then_inc(S["part1_r"], 1)
                dve.tensor_tensor(hot2[:], hot2[:], spread(share2[:], BATCH, EXPERTS), ALU.mult).then_inc(S["part2_r"], 1)
                dve.wait_ge(S["part1_r"], p + 1)
                dve.wait_ge(S["part2_r"], p + 1)
                if not first(p):
                    dve.wait_ge(S["gates_T"], p)
                dve.tensor_tensor(gates[:], hot1[:], hot2[:], ALU.add).then_inc(S["gates_r"], 1)

            def gate_hidden(p):
                dve.wait_ge(S["hidden_r1"], p + 1)
                dve.wait_ge(S["gate_wide_in"], p * 32 + 32)
                if not first(p):
                    dve.wait_ge(S["moe_z"], p)
                dve.tensor_tensor(gated_h[:], hidden[:], gate_wide[:], ALU.mult).then_inc(S["gated_h_r"], 1)

            def mask_scores(p):
                if first(p):
                    dve.wait_ge(S["const_in"], 16)
                dve.wait_ge(S["scores_z"], p + 1)
                if not first(p):
                    dve.wait_ge(S["y_z"], p)
                causal = C["causal"].rearrange("p (o i) -> p o i", o=1).to_broadcast([P, BATCH * CHUNKS, CHUNK])
                for h in range(2):
                    for i in (2 * h, 2 * h + 1):
                        ins = dve.tensor_tensor(masked[:, i].rearrange("p b k i -> p (b k) i"),
                                                scores[:, i, :].rearrange("p (n i) -> p n i", i=CHUNK), causal, ALU.mult)
                    ins.then_inc(S["masked_r"], 1)

            def state_out(p, k):
                dve.wait_ge(S[f"state_k{k}"], p + 1)
                dst, done = ((state_b, "state_b_r"), (state_a, "state_a_r"))[k]
                if k == 0 and not first(p):
                    dve.wait_ge(S["y_z"], p)
                same = C["same_head"].rearrange("p (o d) -> p o d", o=1).to_broadcast([P, BATCH, DIM])
                dve.tensor_tensor(dst[:], bank_s.rearrange("p (b d) -> p b d", b=BATCH), same, ALU.mult).then_inc(S[done], 1)

            def group_centre(p):
                dve.wait_ge(S["y_z"], p + 1)
                y = bank_y.rearrange("p (g d) -> p g d", d=HEAD)
                if not first(p):
                    dve.wait_ge(S["y_norm_r"], p)
                    dve.wait_ge(S["y_sq_r"], p)
                dve.tensor_reduce(y_sum[:], y, AX.X, ALU.add).then_inc(S["y_sum_r"], 1)
                dve.wait_ge(S["y_sum_r"], p + 1)
                dve.scalar_tensor_tensor(y_mid[:], spread(y_sum[:], BATCH * HEADS, HEAD), -1.0 / HEAD, y, ALU.mult,
                                         ALU.add).then_inc(S["y_mid_r"], 1)

            def group_variance(p):
                dve.wait_ge(S["y_sq_r"], p + 1)
                if not first(p):
                    dve.wait_ge(S["y_vare_r"], p)
                dve.tensor_reduce(y_var[:], y_sq[:], AX.X, ALU.add).then_inc(S["y_var_r"], 1)

            def group_norm(p):
                dve.wait_ge(S["y_rstd_r"], p + 1)
                dve.wait_ge(S["y_mid_r"], p + 1)
                dve.tensor_tensor(y_norm[:], y_mid[:], spread(y_rstd[:], BATCH * HEADS, HEAD), ALU.mult).then_inc(S["y_norm_r"], 1)

            def moe_out(p):
                dve.wait_ge(S["sig_moe_r"], p + 1)
                if not first(p):
                    dve.wait_ge(S["update_r"], p)
                dve.scalar_tensor_tensor(moe_silu[:], bank_dv[:, 256:512], 0.5, sig_moe[:], ALU.mult,
                                         ALU.mult).then_inc(S["moe_silu_r"], 1)

            def combine(p):
                dve.wait_ge(S["ret_z"], p + 1)
                dve.wait_ge(S["moe_silu_r"], p + 1)
                dve.wait_ge(S["y_rstd_r"], p + 1)
                dve.tensor_tensor(update[:].rearrange("p b d -> p (b d)"), bank_t, moe_silu[:],
                                  ALU.mult).then_inc(S["update_r"], 1)

            def step(s):
                z, a, b, c, d = s + 1, s, s - 1, s - 2, s - 3
                if live(d):
                    group_norm(d)
                if live(c):
                    weigh(c)
                if live(z):
                    norm0_stats(z)
                if live(a):
                    recurrence(a)
                if live(c):
                    mask_scores(c)
                if live(a):
                    residual0(a)
                if live(c):
                    state_out(c, 0)
                if live(d):
                    combine(d)
                if live(a):
                    norm1(a)
                if live(z):
                    norm0(z)
                if live(c):
                    state_out(c, 1)
                    group_centre(c)
                    gate_hidden(c)
                if live(b):
                    rotate(b)
                if live(c):
                    group_variance(c)
                if live(b):
                    gate_silu(b)
                    choose_first(b)
                if live(c):
                    moe_out(c)
                if live(b):
                    choose_second(b)

            all_steps(dve, step)

        @block.gpsimd
        def _(pool):
            pool.memset(zeros[:], 0.0).then_inc(S["zeros_set"], 1)
            pool.memset(state_a[:], 0.0).then_inc(S["state_set"], 1)
            pool.memset(neg_half[:], -0.5).then_inc(S["neg_half_set"], 1)

            def inverse_root(p, moments, var, rstd, n):
                pool.wait_ge(S["neg_half_set"], 1)
                pool.wait_ge(S[f"moments{n}_r"], p + 1)
                pool.tensor_scalar(var[:], moments[:, :, 1], EPS, 1.0, ALU.add, ALU.mult).then_inc(S[f"var{n}_r"], 1)
                pool.wait_ge(S[f"var{n}_r"], p + 1)
                if not first(p):
                    pool.wait_ge(S[f"xn{n}_r"], p)
                pool.tensor_tensor(rstd[:], var[:], neg_half[:, 0:BATCH], ALU.pow).then_inc(S[f"rstd{n}_r"], 1)

            def gate0(p):
                pool.wait_ge(S["scan_r"], p * 2 + 2)
                pool.wait_ge(S["ffn_silu_r"], p + 1)
                if not first(p):
                    pool.wait_ge(S["gated0_T"], p)
                pool.tensor_tensor(gated0[:], scan[:].rearrange("p b t -> p (b t)"), ffn_silu[:], ALU.mult).then_inc(S["gated0_r"], 1)

            def rotate(p):
                pool.wait_ge(S["rot2_r"], p + 1)
                if not first(p):
                    pool.wait_ge(S["y_z"], p)
                o = qk[:].rearrange("p b i (c t) -> p (b i c) t", t=2)
                c = by_cos[:].rearrange("p b (c t) -> p (b c) t", t=2)
                n = by_sin[:].rearrange("p b (c t) -> p (b c) t", t=2)
                pool.tensor_tensor(o[:, :, 0], c[:, :, 0], n[:, :, 1], ALU.subtract)
                pool.tensor_tensor(o[:, :, 1], c[:, :, 1], n[:, :, 0], ALU.add).then_inc(S["qk_r"], 1)

            def split_v(p):
                pool.wait_ge(S["v_twice_r"], p + 1)
                if first(p):
                    pool.wait_ge(S["const_in"], 16)
                else:
                    pool.wait_ge(S["y_z"], p)
                own = C["own_heads"].rearrange("p (o d) -> p o d", o=1).to_broadcast([P, BATCH * CHUNKS, DIM])
                pool.tensor_tensor(v_split[:].rearrange("p b k d -> p (b k) d"),
                                   v_twice[:].rearrange("p b k d -> p (b k) d"), own, ALU.mult).then_inc(S["v_split_r"], 1)

            def group_square(p):
                pool.wait_ge(S["y_mid_r"], p + 1)
                if not first(p):
                    pool.wait_ge(S["y_var_r"], p)
                pool.tensor_tensor(y_sq[:], y_mid[:], y_mid[:], ALU.mult).then_inc(S["y_sq_r"], 1)

            def group_root(p):
                pool.wait_ge(S["neg_half_set"], 1)
                pool.wait_ge(S["y_var_r"], p + 1)
                pool.tensor_scalar(y_vare[:], y_var[:], 1.0 / HEAD, EPS, ALU.mult, ALU.add).then_inc(S["y_vare_r"], 1)
                pool.wait_ge(S["y_vare_r"], p + 1)
                if not first(p):
                    pool.wait_ge(S["y_norm_r"], p)
                pool.tensor_tensor(y_rstd[:], y_vare[:], neg_half[:], ALU.pow).then_inc(S["y_rstd_r"], 1)

            def group_out(p):
                pool.wait_ge(S["y_norm_r"], p + 1)
                pool.wait_ge(S["g_b_r"], p + 1)
                pool.tensor_tensor(y_w[:].rearrange("p b d -> p (b d)"), y_norm[:].rearrange("p g d -> p (g d)"),
                                   g_w[:].rearrange("p b d -> p (b d)"), ALU.mult).then_inc(S["y_w_r"], 1)
                pool.wait_ge(S["y_w_r"], p + 1)
                pool.wait_ge(S["y_mid_r"], p + 1)
                pool.tensor_tensor(gated_y[:].rearrange("p b d -> p (b d)"), y_w[:].rearrange("p b d -> p (b d)"),
                                   g_b[:].rearrange("p b d -> p (b d)"), ALU.add).then_inc(S["gated_y_r"], 1)

            def gate_affine(p):
                if first(p):
                    pool.wait_ge(S["w1_in"], 16)
                pool.wait_ge(S["g_silu_r"], p + 1)
                if not first(p):
                    pool.wait_ge(S["gated_y_r"], p)
                wide = lambda a: a.rearrange("p (o d) -> p o d", o=1).to_broadcast([P, BATCH, DIM])
                pool.tensor_tensor(g_w[:], g_silu[:], wide(V["gn_w"]), ALU.mult).then_inc(S["g_w_r"], 1)
                pool.tensor_tensor(g_b[:], g_silu[:], wide(V["gn_b"]), ALU.mult).then_inc(S["g_b_r"], 1)

            def residual1(p):
                pool.wait_ge(S["update_r"], p + 1)
                pool.tensor_tensor(both(out_sb, p), update[:], both(x1_sb, p), ALU.add).then_inc(S["out_r"], 1)

            def step(s):
                z, a, b, c, d = s + 1, s, s - 1, s - 2, s - 3
                if live(d):
                    group_out(d)
                if live(c):
                    split_v(c)
                if live(a):
                    gate0(a)
                if live(c):
                    gate_affine(c)
                if live(a):
                    inverse_root(a, moments1, var1, rstd1, 1)
                if live(z):
                    inverse_root(z, moments0, var0, rstd0, 0)
                if live(d):
                    residual1(d)
                if live(c):
                    group_square(c)
                if live(b):
                    rotate(b)
                if live(c):
                    group_root(c)

            all_steps(pool, step)


def kernel(L0_attn_seq, L0_attn_W_delta, L0_attn_b_delta, L0_attn_W_value, L0_attn_b_value, L0_ffn_weight,
           L0_ffn_alpha, L0_ffn_bias, L1_attn_W_Q, L1_attn_W_K, L1_attn_W_V, L1_attn_W_G, L1_attn_W_O,
           L1_attn_gn_weight, L1_attn_gn_bias, L1_ffn_w_gate, L1_ffn_w_noise, L1_ffn_Wd, L1_ffn_bd, L1_ffn_Wu,
           L1_ffn_bu):
    import concourse.bacc as bacc
    from concourse.bass_utils import run_bass_kernel_spmd

    heads = lambda w: np.asarray(w).transpose(1, 0, 2).reshape(DIM, DIM)
    rows = lambda v: np.broadcast_to(np.asarray(v)[None, :], (P, len(v)))
    bu = np.zeros((P, DIM), np.float32)
    bu[:EXPERTS] = L1_ffn_bu
    w0 = np.concatenate([
        np.asarray(L0_attn_W_delta).T, np.asarray(L0_attn_W_value).T, np.asarray(L0_ffn_weight).T,
        np.asarray(L0_attn_b_delta)[:, None], np.asarray(L0_attn_b_value)[:, None],
        np.asarray(L0_ffn_bias)[:, None], rows(L0_ffn_alpha)], axis=1)
    w1 = np.concatenate([
        heads(L1_attn_W_Q), heads(L1_attn_W_K), heads(L1_attn_W_V), L1_attn_W_G, L1_ffn_w_gate, L1_attn_W_O,
        np.asarray(L1_ffn_Wd).transpose(1, 0, 2).reshape(DIM, EXPERTS * NECK),
        np.asarray(L1_ffn_Wu).reshape(DOWN, P, DIM).transpose(1, 0, 2).reshape(P, DOWN * DIM),
        np.asarray(L1_ffn_bd).reshape(DOWN, P).T, bu, rows(L1_attn_gn_weight), rows(L1_attn_gn_bias)], axis=1)
    const, tables = constants()
    nc = bacc.Bacc("TRN2", target_bir_lowering=False, num_devices=1)
    arrays = {"x": np.asarray(L0_attn_seq), "w0": w0, "w1": w1, "const": const, "tables": tables}
    arrays = {k: np.ascontiguousarray(v) for k, v in arrays.items()}
    args = [nc.dram_tensor(k, v.shape, F32, kind="ExternalInput").ap() for k, v in arrays.items()]
    gate_rows = nc.dram_tensor("gate_rows", (EXPERTS, BATCH * P), F32, kind="Internal").ap()
    out = nc.dram_tensor("out", (BATCH, SEQ, DIM), F32, kind="ExternalOutput").ap()
    two_layers(nc, *args, gate_rows, out)
    r = run_bass_kernel_spmd(nc, [arrays], core_ids=[0])
    return r.results[0]["out"]
```

```python
from contextlib import ExitStack

import numpy as np
import concourse.bass as bass
from concourse import mybir

F32 = mybir.dt.float32
F32R = mybir.dt.float32r
ALU = mybir.AluOpType
ACT = mybir.ActivationFunctionType
AX = mybir.AxisListType

P = 128
BATCH, SEQ, DIM = 2, 1024, 128
PAIRS = SEQ // P
HEADS, HEAD = 8, 16
CHUNK = 64
CHUNKS = P // CHUNK
STRIPES = 4
EXPERTS, NECK = 8, 64
DOWN = EXPERTS * NECK // P
EPS = 1e-5
LAG = 3
PEEL = 3

W_PARTS = [("delta", DIM), ("value", DIM), ("ffn", DIM), ("b_delta", 1), ("b_value", 1), ("b_ffn", 1),
           ("alpha", 1)]
V_PARTS = [("qk", 2 * DIM), ("v", DIM), ("g_logit", DIM + EXPERTS), ("o", DIM),
           ("down", EXPERTS * NECK), ("up", DOWN * DIM), ("b_down", DOWN), ("b_up", DIM),
           ("gn_w", DIM), ("gn_b", DIM)]
C_PARTS = [("identity", P), ("causal", CHUNK), ("same_head", DIM), ("even_head", 1), ("odd_head", 1),
           ("descending", BATCH * EXPERTS)]


def columns(parts):
    at, out = 0, {}
    for name, n in parts:
        out[name] = (at, at + n)
        at += n
    return out, at


W_AT, W_N = columns(W_PARTS)
V_AT, V_N = columns(V_PARTS)
C_AT, C_N = columns(C_PARTS)


def constants():
    c = np.zeros((P, C_N), np.float32)
    r = np.arange(P)
    put = lambda name, a: c.__setitem__((slice(None), slice(*C_AT[name])), a)
    put("identity", np.eye(P))
    put("causal", np.arange(CHUNK)[None, :] >= (r % CHUNK)[:, None])
    put("same_head", (r // HEAD)[:, None] == (np.arange(DIM) // HEAD)[None, :])
    put("even_head", (r // HEAD % 2 == 0)[:, None])
    put("odd_head", (r // HEAD % 2 == 1)[:, None])
    put("descending", np.tile(np.arange(EXPERTS, 0, -1), BATCH)[None, :])
    f = np.float32
    half = HEAD // 2
    scale = (np.arange(0, HEAD, 2, dtype=f) + f(0.4 * HEAD)) / f(1.4 * HEAD)
    gamma = (1.0 - np.exp(np.linspace(np.log(1 / 32), np.log(1 / 64), HEADS))).astype(f)
    pos = np.arange(SEQ, dtype=f)
    freq = (f(1.0) / f(10000.0) ** (np.arange(half, dtype=f) / f(half))).astype(f)
    angle = (pos[:, None] * freq[None, :]).astype(f).astype(np.float64)
    mid = pos.astype(np.float64) - SEQ // 2
    grow = (scale.astype(np.float64)[None, None, :] ** (mid[:, None, None] / 64.0)
            * gamma.astype(np.float64)[None, :, None] ** mid[:, None, None])
    both = np.stack([grow, 1.0 / grow], 1)
    tables = np.stack([both * np.cos(angle)[:, None, None, :], both * np.sin(angle)[:, None, None, :]], 1)
    tables = tables.reshape(PAIRS, P, 2, DIM).transpose(1, 0, 2, 3)
    return c, np.ascontiguousarray(tables.astype(f))


def spread_selector():
    return np.repeat(np.eye(P, EXPERTS, dtype=np.float32), NECK, axis=1)


def two_layers(nc, x, w0, w1, const, tables, selector, gate_rows, out):
    with ExitStack() as ctx:
        def sb(name, *shape):
            return ctx.enter_context(nc.sbuf_tensor(name, [P, *shape], F32))

        def sb_split(name, *shape):
            return [ctx.enter_context(nc.sbuf_tensor(name + part, [P, *shape], F32R)) for part in ("_high", "_low")]

        def sem(name):
            return ctx.enter_context(nc.semaphore(name))

        x_sb = sb("x_sb", BATCH, PAIRS, DIM)
        x1_sb = sb("x1_sb", BATCH, PAIRS, DIM)
        out_sb = sb("out_sb", BATCH, PAIRS, DIM)
        tab = sb("tab", PAIRS, 2, DIM)
        w0_sb = sb("w0_sb", W_N)
        w1_sb = sb("w1_sb", V_N)
        c_sb = sb("c_sb", C_N)
        W = {k: w0_sb[:, a:b] for k, (a, b) in W_AT.items()}
        V = {k: w1_sb[:, a:b] for k, (a, b) in V_AT.items()}
        C = {k: c_sb[:, a:b] for k, (a, b) in C_AT.items()}
        abs_sum = sb("abs_sum", 1)
        ones = sb("ones", P)
        table_load = sb("table_load", 1)
        zeros = sb("zeros", BATCH * DIM)
        threshold = sb("threshold", 2)
        v_sum = sb("v_sum", HEADS)
        w_v = sb("w_v", DIM)
        w_qk = sb_split("w_qk", 2 * DIM)
        w_g = sb_split("w_g", DIM + EXPERTS)
        w_down = sb_split("w_down", EXPERTS * NECK)
        split_weights = {"qk": w_qk, "g_logit": w_g, "down": w_down}
        above = sb("above", DIM)
        below = sb("below", DIM)
        w_tern = sb("w_tern", DIM)
        neg_b_delta = sb("neg_b_delta", 1)
        neg_half = sb("neg_half", BATCH * HEADS)
        stats0 = sb("stats0", BATCH, 6)
        moments0 = sb("moments0", BATCH, 2)
        var0 = sb("var0", BATCH)
        rstd0 = sb("rstd0", BATCH)
        xn0 = sb("xn0", BATCH, DIM)
        xn0T = sb("xn0T", BATCH * P)
        keep = sb("keep", BATCH * P)
        delta = sb("delta", BATCH * P)
        sig_ffn = sb("sig_ffn", BATCH * P)
        drive = sb("drive", BATCH * P)
        carry = sb("carry", BATCH)
        scan = sb("scan", BATCH, P)
        ffn_silu = sb("ffn_silu", BATCH * P)
        gated0 = sb("gated0", BATCH * P)
        stats1 = sb("stats1", BATCH, 6)
        moments1 = sb("moments1", BATCH, 2)
        var1 = sb("var1", BATCH)
        rstd1 = sb("rstd1", BATCH)
        xn1 = sb("xn1", BATCH, DIM)
        xn1T = sb_split("xn1T", BATCH * P)
        xn1T_first = sb("xn1T_first", BATCH * P)
        xn1T_twice = sb("xn1T_twice", BATCH * CHUNKS, 2, CHUNK)
        by_cos = sb("by_cos", BATCH, 2 * DIM)
        by_sin = sb("by_sin", BATCH, 2 * DIM)
        qk = sb("qk", BATCH, 2, DIM)
        v_twice = sb("v_twice", BATCH, CHUNKS, DIM)
        v_split = sb("v_split", BATCH, CHUNKS, DIM)
        qT = sb("qT", BATCH * P)
        kT = sb("kT", BATCH, CHUNKS, 2, CHUNK)
        q_wide = sb("q_wide", BATCH, CHUNKS, STRIPES, CHUNK)
        sig_g = sb("sig_g", BATCH, DIM)
        g_silu = sb("g_silu", BATCH, DIM)
        g_w = sb("g_w", BATCH, DIM)
        g_b = sb("g_b", BATCH, DIM)
        logits = sb("logits", BATCH, EXPERTS)
        top1 = sb("top1", BATCH)
        top2 = sb("top2", BATCH)
        is_top = sb("is_top", BATCH, EXPERTS)
        first_at = sb("first_at", BATCH)
        hot1 = sb("hot1", BATCH, EXPERTS)
        rest = sb("rest", BATCH, EXPERTS)
        hot2 = sb("hot2", BATCH, EXPERTS)
        margin = sb("margin", BATCH)
        share1 = sb("share1", BATCH)
        share2 = sb("share2", BATCH)
        gates = sb("gates", BATCH, EXPERTS)
        gatesT = sb("gatesT", BATCH * P)
        gate_wide = sb("gate_wide", DOWN, BATCH * P)
        hidden = sb("hidden", DOWN, BATCH * P)
        gated_h = sb("gated_h", DOWN, BATCH * P)
        sel_sb = sb("sel_sb", EXPERTS * NECK)
        masked = sb("masked", BATCH, CHUNKS, STRIPES, CHUNK)
        state_a = sb("state_a", BATCH, DIM)
        state_b = sb("state_b", BATCH, DIM)
        y_sq = sb("y_sq", BATCH * HEADS, HEAD)
        y_var = sb("y_var", BATCH * HEADS)
        y_vare = sb("y_vare", BATCH * HEADS)
        y_rstd = sb("y_rstd", BATCH * HEADS)
        y_root = sb("y_root", BATCH * HEADS)
        eps = sb("eps", 1)
        y_norm = sb("y_norm", BATCH * HEADS, HEAD)
        y_w = sb("y_w", BATCH * HEADS, HEAD)
        gated_y = sb("gated_y", BATCH, DIM)
        gated_yT = sb("gated_yT", BATCH * P)
        sig_moe = sb("sig_moe", BATCH * DIM)
        moe_silu = sb("moe_silu", BATCH * DIM)
        update = sb("update", BATCH, DIM)

        ps = ctx.enter_context(nc.psum_tensor("ps", [P, 8, 512], F32))
        bank_t = ps[:, 0, 0:256]
        bank_x = ps[:, 0, 256:512]
        bank_dv = ps[:, 1, :]
        bank_up = lambda p: bank_dv[:, 256:512] if isinstance(p, int) and p == PAIRS - 1 else bank_x
        bank_f = ps[:, 2, :]
        g_logits = bank_f[:, 0:BATCH * (DIM + EXPERTS)].rearrange("p (b n) -> p b n", b=BATCH)
        bank_qk = ps[:, 3, :]
        bank_v = ps[:, 4, :]
        bank_qkT = ps[:, 5, :]
        bank_y = ps[:, 6, 0:256]
        bank_s = ps[:, 7, 0:256]
        scores = ps[:, 5:7, :]

        names = """x_first x_next x_rest w0_in w1_early_in w1_late_in const_in tab_first_in tab_in ones_set zeros_set carry_set state_set v_split_set q_wide_set
            neg_half_set eps_set selector_in wide_z y_root_r abs_sum_r abs_total threshold_m threshold_r above_r below_r tern_sign tern_r neg_b_r v_sum_r w_v_r
            stats0_r moments0_r var0_r rstd0_r xn0_r xn0_T xn0T_r dv_z ffn_z keep_r delta_r sig_ffn_r drive_r
            scan_r carry_r ffn_silu_r gated0_r gated0_T x1_r stats1_r moments1_r var1_r rstd1_r xn1_r xn1_T
            xn1T_r xn1T_twice_r xn1T_low_r w1_high_r w1_low_r qk_z v_z g_z rot1_r rot2_r qk_r v_twice_r v_split_r qk_T qT_r kT_r q_wide_r sig_g_r g_silu_r g_w_r g_b_r
            logits_r top1_r istop1_r firstkey1_r first1_r hot1_r rest_r top2_r istop2_r firstkey2_r
            first2_r hot2_r margin_r share1_r share2_r part1_r part2_r gates_r gates_T gatesT_r gatesT_set gate_rows_w
            gate_wide_in down_z0 down_z1 hidden_r0 hidden_r1 gated_h_r bias_z moe_z scores_z masked_r state_k0
            state_b_r state_k1 state_a_r y_z y_sq_r y_var_r y_vare_r y_rstd_r y_norm_r y_w_r
            gated_y_r gated_y_T gated_yT_r ret_z sig_moe_r moe_silu_r update_r out_r out_w""".split()
        S = {n: sem(n) for n in names}

        def live(p):
            return not isinstance(p, int) or 0 <= p < PAIRS

        def first(p):
            return isinstance(p, int) and p == 0

        def last(p):
            return isinstance(p, int) and p == PAIRS - 1

        def at_least(p, n):
            return not isinstance(p, int) or p >= n

        def through(p):
            return min(p + 1, PAIRS) if isinstance(p, int) else p + 1

        def all_steps(engine, step):
            for s in range(-1, PEEL):
                step(s)
            with engine.Fori(PEEL + 2, PAIRS + 1) as count:
                step(count - 2)
            for s in range(PAIRS - 1, PAIRS + LAG):
                step(s)

        def pair(buffer, b, p):
            return buffer[:, b, p, :] if isinstance(p, int) else buffer[:, b, bass.ds(p, 1), :]

        def both(buffer, p):
            return buffer[:, :, p, :] if isinstance(p, int) else buffer[:, :, bass.ds(p, 1), :]

        def spread(ap, n, m):
            return ap.rearrange("p (n o) -> p n o", o=1).to_broadcast([P, n, m])

        block = ctx.enter_context(nc.Block())

        @block.sync
        def _(sp):
            x_in = x.rearrange("b (p t) d -> t b p d", t=P)
            sp.dma_start(x_sb[:, :, 0:1, :], x_in[:, :, 0:1, :]).then_inc(S["x_first"], 16)
            sp.dma_start(w0_sb[:], w0).then_inc(S["w0_in"], 16)
            for b in range(BATCH):
                sp.dma_start(x_sb[:, b, 1:3, :], x_in[:, b, 1:3, :]).then_inc(S["x_next"], 16)
            early = V_AT["g_logit"][1]
            sp.dma_start(w1_sb[:, 0:early], w1[:, 0:early]).then_inc(S["w1_early_in"], 16)
            sp.dma_start(tab[:, 0:1], tables[:, 0:1]).then_inc(S["tab_first_in"], 16)
            sp.dma_start(w1_sb[:, early:], w1[:, early:]).then_inc(S["w1_late_in"], 16)
            sp.dma_start(tab[:, 1:], tables[:, 1:]).then_inc(S["tab_in"], 16)
            for b in range(BATCH):
                sp.dma_start(x_sb[:, b, 3:PAIRS, :], x_in[:, b, 3:PAIRS, :]).then_inc(S["x_rest"], 16)
            sp.dma_start(sel_sb[:], selector).then_inc(S["selector_in"], 16)

            def spread_gates(p):
                sp.wait_ge(S["gatesT_r"], p + 1)
                if not first(p):
                    sp.wait_ge(S["gate_wide_in"], p * 32)
                sp.dma_start(gate_rows, gatesT[0:EXPERTS, :]).then_inc(S["gate_rows_w"], 16)
                sp.wait_ge(S["gate_rows_w"], p * 16 + 16)
                if not first(p):
                    sp.wait_ge(S["gated_h_r"], p)
                rows = gate_rows.rearrange("(c h) t -> h c t", h=2)
                for h in range(2):
                    src = rows[h].rearrange("(o c) t -> o c t", o=1).to_broadcast([NECK, DOWN, BATCH * P])
                    sp.dma_start(gate_wide[NECK * h:NECK * (h + 1)], src).then_inc(S["gate_wide_in"], 16)

            def store(p):
                sp.wait_ge(S["out_r"], p + 1)
                o = out.rearrange("b (p t) d -> t b p d", t=P)
                for b in range(BATCH):
                    if isinstance(p, int):
                        dst = o[:, b, p, :]
                    else:
                        dst = o[:, b, bass.ds(p, 1), :]
                    sp.dma_start(dst, pair(out_sb, b, p)).then_inc(S["out_w"], 16)

            def step(s):
                if live(s - 2) and not last(s - 2):
                    spread_gates(s - 2)
                if live(s - 3):
                    store(s - 3)

            all_steps(sp, step)
            sp.wait_ge(S["out_w"], 16 * BATCH * PAIRS)

        @block.tensor
        def _(pe):
            half = lambda b: slice(b * P, (b + 1) * P)

            def split_product(dst, left, right):
                pe.matmul(dst, left[0], right[1], start=True, stop=False)
                pe.matmul(dst, left[1], right[0], start=False, stop=False)
                return pe.matmul(dst, left[0], right[0], start=False, stop=True)

            pe.wait_ge(S["ones_set"], 1)
            pe.wait_ge(S["abs_sum_r"], 1)
            pe.matmul(bank_f[:, 0:1], ones[:], abs_sum[:], start=True, stop=True).then_inc(S["abs_total"], 1)
            pe.wait_ge(S["const_in"], 16)

            def turn_y(p):
                pe.wait_ge(S["gated_y_r"], p + 1)
                if not (isinstance(p, int) and p == PAIRS - 1):
                    pe.wait_ge(S["moe_silu_r"], p + 1)
                for b in range(BATCH):
                    mm = pe.transpose(bank_t[:, half(b)], gated_y[:, b, :], C["identity"])
                mm.then_inc(S["gated_y_T"], 1)

            def turn_x(p):
                pe.wait_ge(S["xn0_r"], p + 1)
                if at_least(p, 2):
                    pe.wait_ge(S["xn1T_r"], p - 1)
                if at_least(p, 4):
                    pe.wait_ge(S["update_r"], p - 3)
                for b in range(BATCH):
                    mm = pe.transpose(bank_x[:, half(b)], xn0[:, b, :], C["identity"])
                mm.then_inc(S["xn0_T"], 1)

            def output(p):
                pe.wait_ge(S["gated_yT_r"], p + 1)
                for b in range(BATCH):
                    mm = pe.matmul(bank_t[:, half(b)], gated_yT[:, half(b)], V["o"], start=True, stop=True)
                mm.then_inc(S["ret_z"], 1)

            def project0(p):
                pe.wait_ge(S["xn0T_r"], p + 1)
                if first(p):
                    pe.wait_ge(S["w0_in"], 16)
                if not first(p):
                    pe.wait_ge(S["x1_r"], p)
                pe.matmul(bank_dv[:, 0:256], W["delta"], xn0T[:], start=True, stop=True)
                pe.matmul(bank_dv[:, 256:512], W["value"], xn0T[:], start=True, stop=True).then_inc(S["dv_z"], 1)

            def project_ffn(p):
                if first(p):
                    pe.wait_ge(S["tern_r"], 1)
                if at_least(p, 2):
                    pe.wait_ge(S["g_silu_r"], p - 1)
                    pe.wait_ge(S["logits_r"], p - 1)
                pe.matmul(bank_f[:, 0:256], w_tern[:], xn0T[:], start=True, stop=True).then_inc(S["ffn_z"], 1)

            def turn_gated0(p):
                pe.wait_ge(S["gated0_r"], p + 1)
                for b in range(BATCH):
                    mm = pe.transpose(bank_dv[:, half(b)], gated0[:, half(b)], C["identity"])
                mm.then_inc(S["gated0_T"], 1)

            def turn_x1(p):
                pe.wait_ge(S["xn1_r"], p + 1)
                pe.wait_ge(S["xn0T_r"], through(p + 1))
                if at_least(p, 3):
                    pe.wait_ge(S["update_r"], p - 2)
                for b in range(BATCH):
                    mm = pe.transpose(bank_t[:, half(b)], xn1[:, b, :], C["identity"])
                mm.then_inc(S["xn1_T"], 1)

            def project_qk(p):
                if first(p):
                    pe.wait_ge(S["w1_early_in"], 16)
                pe.wait_ge(S["xn1T_r"], p + 1)
                if not first(p):
                    pe.wait_ge(S["xn1T_low_r"], p)
                    pe.wait_ge(S["w1_high_r"], 2)
                    pe.wait_ge(S["w1_low_r"], 2)
                if not first(p):
                    pe.wait_ge(S["hidden_r1"], p)
                for b in range(BATCH):
                    dst = bank_qk[:, b * 256:b * 256 + 256]
                    if first(p):
                        mm = pe.matmul(dst, xn1T_first[:, half(b)], V["qk"], start=True, stop=True)
                    else:
                        mm = split_product(dst, [part[:, half(b)] for part in xn1T], [part[:] for part in w_qk])
                mm.then_inc(S["qk_z"], 1)

            def project_v(p):
                pe.wait_ge(S["xn1T_twice_r"], p + 1)
                if first(p):
                    pe.wait_ge(S["w_v_r"], 1)
                for b in range(BATCH):
                    for k in range(CHUNKS):
                        n = b * CHUNKS + k
                        mm = pe.matmul(bank_v[:, n * DIM:(n + 1) * DIM], xn1T_twice[:, n, :, :].rearrange("p h t -> p (h t)"),
                                       w_v[:], start=True, stop=True)
                mm.then_inc(S["v_z"], 1)

            def project_g(p):
                pe.wait_ge(S["ffn_silu_r"], through(p + 1))
                if not first(p):
                    pe.wait_ge(S["gatesT_r"], p)
                for b in range(BATCH):
                    if first(p):
                        mm = pe.matmul(g_logits[:, b, :], xn1T_first[:, half(b)], V["g_logit"],
                                       start=True, stop=True)
                    else:
                        mm = split_product(g_logits[:, b, :], [part[:, half(b)] for part in xn1T], [part[:] for part in w_g])
                mm.then_inc(S["g_z"], 1)

            def turn_qk(p):
                pe.wait_ge(S["qk_r"], p + 1)
                if not first(p):
                    pe.wait_ge(S["masked_r"], BATCH * p)
                for i in range(2):
                    for b in range(BATCH):
                        mm = pe.transpose(bank_qkT[:, (2 * i + b) * P:(2 * i + b + 1) * P], qk[:, b, i, :],
                                          C["identity"])
                mm.then_inc(S["qk_T"], 1)

            def experts_down(p):
                if first(p):
                    pe.wait_ge(S["w1_late_in"], 16)
                else:
                    pe.wait_ge(S["w1_high_r"], 3)
                    pe.wait_ge(S["w1_low_r"], 3)
                for c in range(DOWN):
                    if c == 2:
                        pe.wait_ge(S["v_split_r"], p + 1)
                    bank = (bank_qk, bank_v)[c // 2]
                    dst = bank[:, (c % 2) * 256:(c % 2) * 256 + 256]
                    if first(p):
                        mm = pe.matmul(dst, V["down"][:, c * P:(c + 1) * P], xn1T_first[:], start=True, stop=True)
                    else:
                        mm = split_product(dst, [part[:, c * P:(c + 1) * P] for part in w_down], [part[:] for part in xn1T])
                    if c % 2:
                        mm.then_inc(S[f"down_z{c // 2}"], 1)

            def turn_gates(p):
                pe.wait_ge(S["gates_r"], p + 1)
                pe.wait_ge(S["g_silu_r"], p + 1)
                pe.wait_ge(S["ffn_silu_r"], through(p + 2))
                for b in range(BATCH):
                    mm = pe.transpose(bank_f[0:EXPERTS, half(b)], gates[:, b, :], C["identity"])
                mm.then_inc(S["gates_T"], 1)

            def spread_last_gates(p):
                pe.wait_ge(S["selector_in"], 16)
                pe.wait_ge(S["gatesT_r"], p + 1)
                pe.wait_ge(S["hidden_r1"], p + 1)
                for c in range(DOWN):
                    mm = pe.matmul((bank_qk, bank_v)[c // 2][:, (c % 2) * 256:(c % 2) * 256 + 256],
                                   sel_sb[:, c * P:(c + 1) * P], gatesT[:], start=True, stop=True)
                mm.then_inc(S["wide_z"], 1)

            def score(p, b):
                if b == 0:
                    pe.wait_ge(S["kT_r"], p + 1)
                    pe.wait_ge(S["q_wide_r"], p + 1)
                    pe.wait_ge(S["qT_r"], p + 1)
                elif not first(p):
                    pe.wait_ge(S["y_w_r"], p)
                for k in range(CHUNKS):
                    mm = pe.matmul(scores[:, b, k * 256:(k + 1) * 256], kT[:, b, k, :, :],
                                   q_wide[:, b, k, :, :].rearrange("p s i -> p (s i)"), start=True, stop=True)
                mm.then_inc(S["scores_z"], 1)

            def add_to_state(p, k):
                rows = slice(64 * k, 64 * k + 64)
                if k == 0:
                    pe.wait_ge(S["v_twice_r"], p + 1)
                    if first(p):
                        pe.wait_ge(S["state_set"], 1)
                        pe.wait_ge(S["zeros_set"], 1)
                        pe.matmul(bank_s, zeros[:, 0:P], zeros[:], start=True, stop=False, skip_group_check=True)
                    else:
                        pe.wait_ge(S["state_a_r"], p)
                else:
                    pe.wait_ge(S["state_b_r"], p + 1)
                for b in range(BATCH):
                    mm = pe.matmul(bank_s[:, b * DIM:(b + 1) * DIM], qk[rows, b, 1, :], v_twice[rows, b, k, :],
                                   start=False, stop=False, skip_group_check=True, tile_position=(64 * k, 0))
                mm.then_inc(S[f"state_k{k}"], 1)

            def read_out(p, k):
                if k == 0:
                    pe.wait_ge(S["masked_r"], BATCH * (p + 1))
                    pe.wait_ge(S["v_split_r"], p + 1)
                else:
                    pe.wait_ge(S["state_b_r"], p + 1)
                rows = slice(64 * k, 64 * k + 64)
                state = (state_a, state_b)[k]
                for b in range(BATCH):
                    at = b * P + k * CHUNK
                    pe.matmul(bank_y[rows, b * DIM:(b + 1) * DIM], qT[:, at:at + CHUNK], state[:, b, :],
                              start=True, stop=False, skip_group_check=True)
                    for i in range(STRIPES):
                        mm = pe.matmul(bank_y[rows, b * DIM + 32 * i:b * DIM + 32 * i + 32],
                                       masked[:, b, k, i, :], v_split[:, b, k, 32 * i:32 * i + 32],
                                       start=False, stop=(i == STRIPES - 1), skip_group_check=True)
                if k == CHUNKS - 1:
                    mm.then_inc(S["y_z"], 1)

            def experts_bias(p):
                pe.wait_ge(S["gatesT_r"], p + 1)
                pe.wait_ge(S["xn1T_r"], through(p + 2))
                pe.wait_ge(S["xn0T_r"], through(p + 3))
                if isinstance(p, int) and p > 0 and not last(p):
                    pe.wait_ge(S["update_r"], p)
                for b in range(BATCH):
                    mm = pe.matmul(bank_up(p)[:, half(b)], gatesT[0:EXPERTS, half(b)], V["b_up"][0:EXPERTS, :],
                                   start=(b == 0), stop=False, skip_group_check=True)
                mm.then_inc(S["bias_z"], 1)

            def experts_up(p):
                pe.wait_ge(S["gated_h_r"], p + 1)
                for b in range(BATCH):
                    for c in range(DOWN):
                        mm = pe.matmul(bank_up(p)[:, half(b)], gated_h[:, c, half(b)], V["up"][:, c * DIM:(c + 1) * DIM],
                                       start=False, stop=(c == DOWN - 1), skip_group_check=True)
                mm.then_inc(S["moe_z"], 1)

            def step(s):
                z, a, b, c, d = s + 1, s, s - 1, s - 2, s - 3
                if live(d) and not live(b):
                    if not last(d):
                        experts_bias(d)
                    experts_up(d)
                if live(c):
                    score(c, 0)
                    if not live(b):
                        turn_gates(c)
                    score(c, 1)
                if live(d) and live(b):
                    experts_bias(d)
                    experts_up(d)
                if live(c):
                    if live(b) and live(d):
                        turn_gates(c)
                    add_to_state(c, 0)
                if live(d) and not live(b):
                    turn_y(d)
                if last(c):
                    spread_last_gates(c)
                if live(b) and not live(c):
                    project_qk(b)
                    project_v(b)
                if live(z) and not live(b):
                    turn_x(z)
                if live(c) and not live(d):
                    project_qk(b)
                if live(a):
                    turn_gated0(a)
                if live(c):
                    if live(b) and live(d):
                        project_qk(b)
                    if not live(d):
                        turn_gates(c)
                    read_out(c, 0)
                    if live(d) and live(b):
                        turn_y(d)
                    if live(b):
                        add_to_state(c, 1)
                    read_out(c, 1)
                    if last(c):
                        experts_bias(c)
                if live(d):
                    output(d)
                if live(b):
                    if live(c) and live(a):
                        project_v(b)
                    project_g(b)
                    if not live(a):
                        project_v(b)
                    if live(z):
                        turn_x(z)
                    turn_qk(b)
                    experts_down(b)
                if live(z):
                    project0(z)
                if live(a):
                    turn_x1(a)
                if live(z):
                    project_ffn(z)

            all_steps(pe, step)

        @block.scalar
        def _(act):
            act.dma_start(c_sb[:], const).then_inc(S["const_in"], 16)
            act.wait_ge(S["zeros_set"], 1)
            act.activation(table_load[:], zeros[:, 0:1], ACT.Sigmoid)

            def norm0_out(p):
                act.wait_ge(S["xn0_T"], p + 1)
                if not first(p):
                    act.wait_ge(S["ffn_z"], p)
                act.copy(xn0T[:], bank_x).then_inc(S["xn0T_r"], 1)

            def sigmoids0(p):
                if first(p):
                    act.wait_ge(S["w0_in"], 16)
                    act.wait_ge(S["neg_b_r"], 1)
                act.wait_ge(S["dv_z"], p + 1)
                if not first(p):
                    act.wait_ge(S["drive_r"], p)
                act.activation(delta[:], bank_dv[:, 0:256], ACT.Sigmoid, bias=W["b_delta"]).then_inc(S["delta_r"], 1)
                if not first(p):
                    act.wait_ge(S["scan_r"], 2 * p)
                act.activation(keep[:], bank_dv[:, 0:256], ACT.Sigmoid, bias=neg_b_delta[:], scale=-1.0).then_inc(S["keep_r"], 1)

            def sigmoid_ffn(p):
                act.wait_ge(S["ffn_z"], p + 1)
                if not first(p):
                    act.wait_ge(S["ffn_silu_r"], p)
                act.activation(sig_ffn[:], bank_f[:, 0:256], ACT.Sigmoid, bias=W["b_ffn"]).then_inc(S["sig_ffn_r"], 1)

            def norm1_out(p):
                act.wait_ge(S["xn1_T"], p + 1)
                if not first(p):
                    act.wait_ge(S["down_z1"], p)
                chunks = bank_t.rearrange("p (n o t) -> p n o t", o=1, t=CHUNK).to_broadcast([P, BATCH * CHUNKS, 2, CHUNK])
                act.copy(xn1T_twice[:], chunks).then_inc(S["xn1T_twice_r"], 1)
                dst = xn1T_first if first(p) else xn1T[0]
                act.copy(dst[:], bank_t).then_inc(S["xn1T_r"], 1)

            def weights_high(names):
                for name in names:
                    act.wait_ge(S["w1_late_in" if name == "down" else "w1_early_in"], 16)
                    act.copy(split_weights[name][0][:], V[name]).then_inc(S["w1_high_r"], 1)

            def last_root(p):
                act.wait_ge(S["eps_set"], 1)
                act.wait_ge(S["y_var_r"], p + 1)
                act.activation(y_root[:], y_var[:], ACT.Sqrt, bias=eps[:], scale=1.0 / HEAD).then_inc(S["y_root_r"], 1)

            def v_out(p):
                act.wait_ge(S["v_z"], p + 1)
                if first(p):
                    act.wait_ge(S["v_split_set"], 1)
                else:
                    act.wait_ge(S["y_z"], p)
                act.copy(v_twice[:].rearrange("p b k d -> p (b k d)"), bank_v).then_inc(S["v_twice_r"], 1)
                for h in range(2):
                    rows = slice(64 * h, 64 * h + 64)
                    of_heads = lambda a: a.rearrange("p (s h d) -> p s h d", h=2, d=HEAD)[:, :, h, :]
                    ins = act.copy(of_heads(v_split[rows].rearrange("p b k d -> p (b k d)")), of_heads(bank_v[rows]))
                ins.then_inc(S["v_split_r"], 1)

            def gate_sigmoid(p):
                act.wait_ge(S["g_z"], p + 1)
                if not first(p):
                    act.wait_ge(S["g_silu_r"], p)
                act.activation(sig_g[:], g_logits[:, :, 0:DIM], ACT.Sigmoid).then_inc(S["sig_g_r"], 1)

            def shares(p):
                act.wait_ge(S["margin_r"], p + 1)
                if not first(p):
                    act.wait_ge(S["gates_r"], p)
                act.activation(share1[:], margin[:], ACT.Sigmoid).then_inc(S["share1_r"], 1)
                act.activation(share2[:], margin[:], ACT.Sigmoid, scale=-1.0).then_inc(S["share2_r"], 1)

            def qk_out(p):
                act.wait_ge(S["qk_T"], p + 1)
                if not first(p):
                    act.wait_ge(S["y_z"], p)
                keys = bank_qkT[:, 256:512].rearrange("p (b k j) -> p (b k) j", b=BATCH, k=CHUNKS)
                spots = kT[:].rearrange("p b k h j -> p (b k) h j")
                act.activation(spots[:, :, 0, :], keys, ACT.Copy, scale=C["even_head"])
                act.activation(spots[:, :, 1, :], keys, ACT.Copy, scale=C["odd_head"]).then_inc(S["kT_r"], 1)
                if first(p):
                    act.wait_ge(S["q_wide_set"], 1)
                for i in range(STRIPES):
                    rows = slice(32 * i, 32 * i + 32)
                    ins = act.copy(q_wide[rows, :, :, i, :].rearrange("p b k j -> p (b k) j"),
                                   bank_qkT[rows, 0:256].rearrange("p (n j) -> p n j", j=CHUNK))
                ins.then_inc(S["q_wide_r"], 1)
                act.copy(qT[:], bank_qkT[:, 0:256]).then_inc(S["qT_r"], 1)

            def gates_out(p):
                if first(p):
                    act.wait_ge(S["gatesT_set"], 1)
                act.wait_ge(S["gates_T"], p + 1)
                if not first(p):
                    act.wait_ge(S["bias_z"], p)
                    act.wait_ge(S["gate_rows_w"], p * 16)
                act.copy(gatesT[0:EXPERTS, :], bank_f[0:EXPERTS, 0:256]).then_inc(S["gatesT_r"], 1)

            def experts_relu(p):
                for c in range(DOWN):
                    if c % 2 == 0:
                        act.wait_ge(S[f"down_z{c // 2}"], p + 1)
                    if c == 0 and not first(p):
                        act.wait_ge(S["gated_h_r"], p)
                    bank = (bank_qk, bank_v)[c // 2]
                    ins = act.activation(hidden[:, c, :], bank[:, (c % 2) * 256:(c % 2) * 256 + 256], ACT.Relu,
                                         bias=V["b_down"][:, c:c + 1])
                    if c % 2:
                        ins.then_inc(S[f"hidden_r{c // 2}"], 1)

            def y_out(p):
                act.wait_ge(S["gated_y_T"], p + 1)
                if isinstance(p, int):
                    if p > 0:
                        act.wait_ge(S["ret_z"], p)
                else:
                    act.wait_ge(S["moe_z"], p + 1)
                act.copy(gated_yT[:], bank_t).then_inc(S["gated_yT_r"], 1)

            def group_square(p):
                act.wait_ge(S["y_z"], p + 1)
                if not first(p):
                    act.wait_ge(S["y_var_r"], p)
                act.activation(y_sq[:].rearrange("p g d -> p (g d)"), bank_y, ACT.Square).then_inc(S["y_sq_r"], 1)

            def moe_sigmoid(p):
                act.wait_ge(S["moe_z"], p + 1)
                act.wait_ge(S["masked_r"], BATCH * (p + 1))
                act.activation(sig_moe[:], bank_up(p), ACT.Sigmoid, scale=0.5).then_inc(S["sig_moe_r"], 1)

            def step(s):
                z, a, b, c, d = s + 1, s, s - 1, s - 2, s - 3
                if live(b) and live(c):
                    norm1_out(b)
                if live(a):
                    sigmoids0(a)
                if live(b) and not live(c):
                    norm1_out(b)
                if live(a):
                    sigmoid_ffn(a)
                if live(c):
                    shares(c)
                    if not live(b):
                        experts_relu(c)
                    if live(b):
                        experts_relu(c)
                        if first(c):
                            weights_high(("down",))
                        gates_out(c)
                if live(d):
                    moe_sigmoid(d)
                if live(c) and not live(b):
                    gates_out(c)
                if live(d):
                    y_out(d)
                if last(c):
                    act.activation(table_load[:], zeros[:, 0:1], ACT.Sqrt)
                if live(c):
                    group_square(c)
                if last(c):
                    last_root(c)
                    act.activation(table_load[:], zeros[:, 0:1], ACT.Sigmoid)
                if live(b):
                    if first(b):
                        weights_high(("qk", "g_logit"))
                    if live(a):
                        v_out(b)
                    gate_sigmoid(b)
                    if not live(a):
                        v_out(b)
                if live(z):
                    norm0_out(z)
                if live(b):
                    qk_out(b)

            all_steps(act, step)

        @block.vector
        def _(dve):
            dve.memset(ones[:], 1.0).then_inc(S["ones_set"], 1)
            dve.memset(carry[:], 0.0).then_inc(S["carry_set"], 1)

            def ternary_mean():
                dve.wait_ge(S["w0_in"], 16)
                dve.tensor_reduce(abs_sum[:], W["ffn"], AX.X, ALU.add, apply_absolute_value=True).then_inc(S["abs_sum_r"], 1)
                dve.tensor_scalar(neg_b_delta[:], W["b_delta"], -1.0, None, ALU.mult).then_inc(S["neg_b_r"], 1)

            def ternary_weights():
                dve.wait_ge(S["abs_total"], 1)
                dve.tensor_scalar(threshold[:, 0:1], bank_f[:, 0:1], 1.0 / (DIM * DIM), 0.7, ALU.mult, ALU.mult).then_inc(S["threshold_m"], 1)
                dve.wait_ge(S["threshold_m"], 1)
                dve.tensor_scalar(threshold[:, 1:2], threshold[:, 0:1], -1.0, None, ALU.mult).then_inc(S["threshold_r"], 1)
                dve.wait_ge(S["threshold_r"], 1)
                dve.tensor_scalar(above[:], W["ffn"], threshold[:, 0:1], None, ALU.is_gt).then_inc(S["above_r"], 1)
                dve.tensor_scalar(below[:], W["ffn"], threshold[:, 1:2], None, ALU.is_lt).then_inc(S["below_r"], 1)
                dve.wait_ge(S["above_r"], 1)
                dve.wait_ge(S["below_r"], 1)
                dve.tensor_tensor(above[:], above[:], below[:], ALU.subtract).then_inc(S["tern_sign"], 1)
                dve.wait_ge(S["tern_sign"], 1)
                dve.tensor_scalar(w_tern[:], above[:], W["alpha"], None, ALU.mult).then_inc(S["tern_r"], 1)

            def centre_values():
                dve.wait_ge(S["w1_early_in"], 16)
                dve.tensor_reduce(v_sum[:], V["v"].rearrange("p (h d) -> p h d", d=HEAD), AX.X, ALU.add).then_inc(S["v_sum_r"], 1)
                dve.wait_ge(S["v_sum_r"], 1)
                dve.scalar_tensor_tensor(w_v[:].rearrange("p (h d) -> p h d", d=HEAD), spread(v_sum[:], HEADS, HEAD), -1.0 / HEAD,
                                         V["v"].rearrange("p (h d) -> p h d", d=HEAD), ALU.mult, ALU.add).then_inc(S["w_v_r"], 1)

            def normalise(p, buffer, moments, rstd, xn, n):
                dve.wait_ge(S[f"rstd{n}_r"], p + 1)
                dve.wait_ge(S[f"moments{n}_r"], p + 1)
                for b in range(BATCH):
                    ins = dve.tensor_scalar(xn[:, b, :], pair(buffer, b, p), moments[:, b, 0:1], rstd[:, b:b + 1],
                                            ALU.subtract, ALU.mult)
                ins.then_inc(S[f"xn{n}_r"], 1)

            def norm0_stats(p, b):
                dve.wait_ge(S["x_first"], 16)
                if b == 0 and not first(p):
                    near = isinstance(p, int) and p < 3
                    dve.wait_ge(S["x_next" if near else "x_rest"], 16 * BATCH)
                ins = dve.bn_stats(stats0[:, b, :], pair(x_sb, b, p))
                if b == BATCH - 1:
                    ins.then_inc(S["stats0_r"], 1)

            def norm0_moments(p):
                dve.wait_ge(S["x_first"], 16)
                dve.wait_ge(S["stats0_r"], p + 1)
                if not first(p):
                    dve.wait_ge(S["xn0_r"], p)
                for b in range(BATCH):
                    ins = dve.bn_aggr(moments0[:, b, :], stats0[:, b, :])
                ins.then_inc(S["moments0_r"], 1)

            def norm0(p):
                if not first(p):
                    dve.wait_ge(S["xn0_T"], p)
                normalise(p, x_sb, moments0, rstd0, xn0, 0)

            def driven(p):
                dve.wait_ge(S["delta_r"], p + 1)
                dve.wait_ge(S["keep_r"], p + 1)
                if not first(p):
                    dve.wait_ge(S["scan_r"], 2 * p)
                dve.scalar_tensor_tensor(drive[:], bank_dv[:, 256:512], W["b_value"], delta[:], ALU.add,
                                         ALU.mult).then_inc(S["drive_r"], 1)

            def recurrence(p, b):
                dve.wait_ge(S["drive_r"], p + 1)
                if first(p):
                    dve.wait_ge(S["carry_set"], 1)
                elif b == 0:
                    dve.wait_ge(S["carry_r"], p)
                    dve.wait_ge(S["gated0_r"], p)
                at = slice(b * P, (b + 1) * P)
                dve.tensor_tensor_scan(scan[:, b, :], keep[:, at], drive[:, at], carry[:, b:b + 1],
                                       ALU.mult, ALU.add).then_inc(S["scan_r"], 1)

            def silu0(p):
                dve.wait_ge(S["sig_ffn_r"], p + 1)
                if not first(p):
                    dve.wait_ge(S["gated0_r"], p)
                dve.scalar_tensor_tensor(ffn_silu[:], bank_f[:, 0:256], W["b_ffn"], sig_ffn[:], ALU.add,
                                         ALU.mult).then_inc(S["ffn_silu_r"], 1)

            def carry_over(p):
                dve.wait_ge(S["scan_r"], p * 2 + 2)
                dve.tensor_copy(carry[:], scan[:, :, P - 1]).then_inc(S["carry_r"], 1)

            def residual0(p):
                dve.wait_ge(S["gated0_T"], p + 1)
                dve.tensor_tensor(both(x1_sb, p), bank_dv[:, 0:256].rearrange("p (b d) -> p b d", b=BATCH), both(x_sb, p),
                                  ALU.add).then_inc(S["x1_r"], 1)

            def norm1_stats(p):
                dve.wait_ge(S["x_first"], 16)
                dve.wait_ge(S["x1_r"], p + 1)
                for b in range(BATCH):
                    ins = dve.bn_stats(stats1[:, b, :], pair(x1_sb, b, p))
                ins.then_inc(S["stats1_r"], 1)

            def norm1_moments(p):
                dve.wait_ge(S["x_first"], 16)
                dve.wait_ge(S["stats1_r"], p + 1)
                if not first(p):
                    dve.wait_ge(S["xn1_r"], p)
                for b in range(BATCH):
                    ins = dve.bn_aggr(moments1[:, b, :], stats1[:, b, :])
                ins.then_inc(S["moments1_r"], 1)

            def norm1(p):
                if not first(p):
                    dve.wait_ge(S["xn1_T"], p)
                normalise(p, x1_sb, moments1, rstd1, xn1, 1)

            def rotate(p):
                if first(p):
                    dve.wait_ge(S["tab_first_in"], 16)
                elif isinstance(p, int) and p == 1:
                    dve.wait_ge(S["tab_in"], 16)
                dve.wait_ge(S["qk_z"], p + 1)
                if not first(p):
                    dve.wait_ge(S["qk_r"], p)
                for i, dst in enumerate((by_cos, by_sin)):
                    t = tab[:, p, i, :] if isinstance(p, int) else tab[:, bass.ds(p, 1), i, :].rearrange("p o d -> p (o d)")
                    for b in range(BATCH):
                        ins = dve.tensor_tensor(dst[:, b, :].rearrange("p (c t) -> p c t", t=2),
                                                bank_qk[:, b * 256:b * 256 + 256].rearrange("p (c t) -> p c t", t=2),
                                                spread(t, DIM, 2), ALU.mult)
                    ins.then_inc(S[f"rot{i + 1}_r"], 1)

            def gate_silu(p):
                dve.wait_ge(S["sig_g_r"], p + 1)
                if not first(p):
                    dve.wait_ge(S["g_b_r"], p)
                dve.tensor_tensor(g_silu[:], g_logits[:, :, 0:DIM], sig_g[:], ALU.mult).then_inc(S["g_silu_r"], 1)

            def logits_out(p):
                dve.wait_ge(S["sig_g_r"], p + 1)
                dve.tensor_copy(logits[:], g_logits[:, :, DIM:]).then_inc(S["logits_r"], 1)

            def largest(p, n):
                dve.wait_ge(S[("logits_r", "rest_r")[n - 1]], p + 1)
                values, top = ((logits, top1), (rest, top2))[n - 1]
                dve.tensor_reduce(top[:], values[:], AX.X, ALU.max).then_inc(S[f"top{n}_r"], 1)

            def where_largest(p, n):
                values, top = ((logits, top1), (rest, top2))[n - 1]
                dve.wait_ge(S[f"top{n}_r"], p + 1)
                dve.tensor_tensor(is_top[:], values[:], spread(top[:], BATCH, EXPERTS), ALU.is_equal).then_inc(S[f"istop{n}_r"], 1)

            def order_keys(p, n):
                dve.wait_ge(S[f"istop{n}_r"], p + 1)
                dve.tensor_tensor(is_top[:], is_top[:], C["descending"].rearrange("p (b e) -> p b e", b=BATCH),
                                  ALU.mult).then_inc(S[f"firstkey{n}_r"], 1)

            def first_key(p, n):
                dve.wait_ge(S[f"firstkey{n}_r"], p + 1)
                dve.tensor_reduce(first_at[:], is_top[:], AX.X, ALU.max).then_inc(S[f"first{n}_r"], 1)

            def one_hot(p, n):
                dve.wait_ge(S[f"first{n}_r"], p + 1)
                hot = (hot1, hot2)[n - 1]
                if n == 1 and not first(p):
                    dve.wait_ge(S["gates_r"], p)
                dve.tensor_tensor(hot[:], is_top[:], spread(first_at[:], BATCH, EXPERTS), ALU.is_equal).then_inc(S[f"hot{n}_r"], 1)

            def without_first(p):
                dve.wait_ge(S["hot1_r"], p + 1)
                dve.scalar_tensor_tensor(rest[:], hot1[:], -3.0e38, logits[:], ALU.mult, ALU.add).then_inc(S["rest_r"], 1)

            def lead(p):
                dve.wait_ge(S["top2_r"], p + 1)
                dve.tensor_tensor(margin[:], top1[:], top2[:], ALU.subtract).then_inc(S["margin_r"], 1)

            def weigh(p):
                dve.wait_ge(S["share1_r"], p + 1)
                dve.wait_ge(S["share2_r"], p + 1)
                dve.wait_ge(S["hot2_r"], p + 1)
                dve.tensor_tensor(hot1[:], hot1[:], spread(share1[:], BATCH, EXPERTS), ALU.mult).then_inc(S["part1_r"], 1)
                dve.tensor_tensor(hot2[:], hot2[:], spread(share2[:], BATCH, EXPERTS), ALU.mult).then_inc(S["part2_r"], 1)
                dve.wait_ge(S["part1_r"], p + 1)
                dve.wait_ge(S["part2_r"], p + 1)
                if not first(p):
                    dve.wait_ge(S["gates_T"], p)
                dve.tensor_tensor(gates[:], hot1[:], hot2[:], ALU.add).then_inc(S["gates_r"], 1)

            def gate_hidden(p):
                dve.wait_ge(S["hidden_r1"], p + 1)
                if last(p):
                    dve.wait_ge(S["wide_z"], 1)
                    wide = ps[:, 3:5, :].rearrange("p o n -> p (o n)").rearrange("p (c t) -> p c t", c=DOWN)
                else:
                    dve.wait_ge(S["gate_wide_in"], p * 32 + 32)
                    wide = gate_wide[:]
                if not first(p):
                    dve.wait_ge(S["moe_z"], p)
                dve.tensor_tensor(gated_h[:], hidden[:], wide, ALU.mult).then_inc(S["gated_h_r"], 1)

            def mask_scores(p, b):
                if first(p):
                    dve.wait_ge(S["const_in"], 16)
                dve.wait_ge(S["scores_z"], BATCH * p + b + 1)
                if b == 0 and not first(p):
                    dve.wait_ge(S["y_z"], p)
                causal = C["causal"].rearrange("p (o i) -> p o i", o=1).to_broadcast([P, CHUNKS * STRIPES, CHUNK])
                dve.tensor_tensor(masked[:, b].rearrange("p k s i -> p (k s) i"),
                                  scores[:, b, :].rearrange("p (n i) -> p n i", i=CHUNK), causal,
                                  ALU.mult).then_inc(S["masked_r"], 1)

            def state_out(p, k):
                dve.wait_ge(S[f"state_k{k}"], p + 1)
                dst, done = ((state_b, "state_b_r"), (state_a, "state_a_r"))[k]
                if k == 0 and not first(p):
                    dve.wait_ge(S["y_z"], p)
                same = C["same_head"].rearrange("p (o d) -> p o d", o=1).to_broadcast([P, BATCH, DIM])
                dve.tensor_tensor(dst[:], bank_s.rearrange("p (b d) -> p b d", b=BATCH), same, ALU.mult).then_inc(S[done], 1)

            def group_weigh(p):
                dve.wait_ge(S["g_w_r"], p + 1)
                dve.wait_ge(S["y_sq_r"], p + 1)
                if not first(p):
                    dve.wait_ge(S["y_norm_r"], p)
                dve.tensor_tensor(y_w[:].rearrange("p g d -> p (g d)"), bank_y, g_w[:].rearrange("p b d -> p (b d)"),
                                  ALU.mult).then_inc(S["y_w_r"], 1)

            def group_variance(p):
                dve.wait_ge(S["y_sq_r"], p + 1)
                if not first(p):
                    dve.wait_ge(S["y_vare_r"], p)
                dve.tensor_reduce(y_var[:], y_sq[:], AX.X, ALU.add).then_inc(S["y_var_r"], 1)

            def last_group_norm(p):
                dve.wait_ge(S["y_root_r"], 1)
                dve.wait_ge(S["y_norm_r"], p)
                dve.reciprocal(y_rstd[:], y_root[:]).then_inc(S["y_rstd_r"], 1)
                dve.wait_ge(S["y_rstd_r"], p + 1)
                dve.wait_ge(S["y_w_r"], p + 1)
                dve.wait_ge(S["gated_y_r"], p)
                dve.tensor_tensor(y_norm[:], y_w[:], spread(y_rstd[:], BATCH * HEADS, HEAD), ALU.mult).then_inc(S["y_norm_r"], 1)
                dve.wait_ge(S["y_norm_r"], p + 1)
                dve.wait_ge(S["g_b_r"], p + 1)
                dve.wait_ge(S["gated_y_T"], p)
                dve.tensor_tensor(gated_y[:].rearrange("p b d -> p (b d)"), y_norm[:].rearrange("p g d -> p (g d)"),
                                  g_b[:].rearrange("p b d -> p (b d)"), ALU.add).then_inc(S["gated_y_r"], 1)

            def last_residual(p):
                dve.wait_ge(S["update_r"], p + 1)
                dve.tensor_tensor(both(out_sb, p), update[:], both(x1_sb, p), ALU.add).then_inc(S["out_r"], 1)

            def moe_out(p):
                dve.wait_ge(S["sig_moe_r"], p + 1)
                dve.wait_ge(S["y_rstd_r"], p + 1)
                dve.scalar_tensor_tensor(moe_silu[:], bank_up(p), 0.5, sig_moe[:], ALU.mult,
                                         ALU.mult).then_inc(S["moe_silu_r"], 1)

            def combine(p):
                dve.wait_ge(S["ret_z"], p + 1)
                dve.wait_ge(S["moe_silu_r"], p + 1)
                if last(p) or last(p + 1):
                    dve.wait_ge(S["out_r"], p)
                else:
                    dve.wait_ge(S["y_rstd_r"], p + 1)
                dve.tensor_tensor(update[:].rearrange("p b d -> p (b d)"), bank_t, moe_silu[:],
                                  ALU.mult).then_inc(S["update_r"], 1)

            def step(s):
                z, a, b, c, d = s + 1, s, s - 1, s - 2, s - 3
                if live(c):
                    largest(c, 1)
                if live(z):
                    norm0_stats(z, 0)
                if live(c):
                    where_largest(c, 1)
                if live(z):
                    norm0_stats(z, 1)
                if live(c):
                    order_keys(c, 1)
                if live(z):
                    norm0_moments(z)
                    if first(z):
                        ternary_mean()
                    if not live(c):
                        norm0(z)
                    if first(z):
                        ternary_weights()
                if live(c):
                    first_key(c, 1)
                    one_hot(c, 1)
                    without_first(c)
                    largest(c, 2)
                    where_largest(c, 2)
                    lead(c)
                if live(a):
                    driven(a)
                if live(c):
                    order_keys(c, 2)
                if live(a):
                    recurrence(a, 0)
                if live(c):
                    first_key(c, 2)
                if live(a):
                    recurrence(a, 1)
                if live(c):
                    one_hot(c, 2)
                if live(a):
                    silu0(a)
                if live(c):
                    weigh(c)
                    if live(d) and not live(b):
                        moe_out(d)
                    mask_scores(c, 0)
                    mask_scores(c, 1)
                if live(a):
                    carry_over(a)
                if live(z):
                    if live(c):
                        norm0(z)
                if live(d) and (live(b) or not live(c)):
                    moe_out(d)
                if live(c):
                    state_out(c, 0)
                if live(b):
                    if not live(c):
                        rotate(b)
                if live(a):
                    residual0(a)
                if live(b):
                    if live(c):
                        rotate(b)
                if live(a):
                    norm1_stats(a)
                    norm1_moments(a)
                if live(c) and live(b):
                    state_out(c, 1)
                if last(c):
                    gate_hidden(c)
                    group_variance(c)
                if live(d) and live(b):
                    combine(d)
                if live(c):
                    group_weigh(c)
                if last(c) or last(d):
                    combine(d)
                if last(c):
                    last_group_norm(c)
                if last(d):
                    last_residual(d)
                if live(c):
                    if live(b):
                        group_variance(c)
                if live(a):
                    norm1(a)
                    if first(a):
                        centre_values()
                if live(b):
                    if not live(a):
                        logits_out(b)
                    gate_silu(b)
                    if live(a):
                        logits_out(b)
                if live(c) and not last(c):
                    gate_hidden(c)

            all_steps(dve, step)

        @block.gpsimd
        def _(pool):
            pool.memset(zeros[:], 0.0).then_inc(S["zeros_set"], 1)
            pool.memset(state_a[:], 0.0).then_inc(S["state_set"], 1)
            pool.memset(v_split[:], 0.0).then_inc(S["v_split_set"], 1)
            pool.memset(q_wide[:], 0.0).then_inc(S["q_wide_set"], 1)
            pool.memset(neg_half[:], -0.5).then_inc(S["neg_half_set"], 1)
            pool.memset(eps[:], EPS).then_inc(S["eps_set"], 1)
            pool.memset(gatesT[:], 0.0).then_inc(S["gatesT_set"], 1)

            def inverse_root(p, moments, var, rstd, n):
                pool.wait_ge(S["neg_half_set"], 1)
                pool.wait_ge(S[f"moments{n}_r"], p + 1)
                pool.tensor_scalar(var[:], moments[:, :, 1], EPS, 1.0, ALU.add, ALU.mult).then_inc(S[f"var{n}_r"], 1)
                pool.wait_ge(S[f"var{n}_r"], p + 1)
                if not first(p):
                    pool.wait_ge(S[f"xn{n}_r"], p)
                pool.tensor_tensor(rstd[:], var[:], neg_half[:, 0:BATCH], ALU.pow).then_inc(S[f"rstd{n}_r"], 1)

            def weights_low(names):
                for name in names:
                    pool.wait_ge(S["w1_late_in" if name == "down" else "w1_early_in"], 16)
                    pool.wait_ge(S["w1_high_r"], list(split_weights).index(name) + 1)
                    high, low = split_weights[name]
                    pool.tensor_tensor(low[:], V[name], high[:].bitcast(F32), ALU.subtract).then_inc(S["w1_low_r"], 1)

            def norm1_low(p):
                pool.wait_ge(S["xn1T_r"], p + 1)
                pool.wait_ge(S["down_z1"], p)
                pool.tensor_tensor(xn1T[1][:].rearrange("p (n t) -> p n t", t=CHUNK), xn1T_twice[:, :, 0, :],
                                   xn1T[0][:].bitcast(F32).rearrange("p (n t) -> p n t", t=CHUNK),
                                   ALU.subtract).then_inc(S["xn1T_low_r"], 1)

            def gate0(p):
                pool.wait_ge(S["scan_r"], p * 2 + 2)
                pool.wait_ge(S["ffn_silu_r"], p + 1)
                if not first(p):
                    pool.wait_ge(S["gated0_T"], p)
                pool.tensor_tensor(gated0[:], scan[:].rearrange("p b t -> p (b t)"), ffn_silu[:], ALU.mult).then_inc(S["gated0_r"], 1)

            def rotate(p):
                pool.wait_ge(S["rot2_r"], p + 1)
                if not first(p):
                    pool.wait_ge(S["state_k1"], p)
                o = qk[:].rearrange("p b i (c t) -> p (b i c) t", t=2)
                c = by_cos[:].rearrange("p b (c t) -> p (b c) t", t=2)
                n = by_sin[:].rearrange("p b (c t) -> p (b c) t", t=2)
                pool.tensor_tensor(o[:, :, 0], c[:, :, 0], n[:, :, 1], ALU.subtract)
                pool.tensor_tensor(o[:, :, 1], c[:, :, 1], n[:, :, 0], ALU.add).then_inc(S["qk_r"], 1)

            def group_root(p):
                pool.wait_ge(S["neg_half_set"], 1)
                pool.wait_ge(S["y_var_r"], p + 1)
                pool.tensor_scalar(y_vare[:], y_var[:], 1.0 / HEAD, EPS, ALU.mult, ALU.add).then_inc(S["y_vare_r"], 1)
                pool.wait_ge(S["y_vare_r"], p + 1)
                if not first(p):
                    pool.wait_ge(S["y_norm_r"], p)
                pool.tensor_tensor(y_rstd[:], y_vare[:], neg_half[:], ALU.pow).then_inc(S["y_rstd_r"], 1)

            def gate_affine(p):
                if first(p):
                    pool.wait_ge(S["w1_late_in"], 16)
                pool.wait_ge(S["g_silu_r"], p + 1)
                if not first(p):
                    pool.wait_ge(S["y_w_r"], p)
                    pool.wait_ge(S["gated_y_r"], p)
                wide = lambda a: a.rearrange("p (o d) -> p o d", o=1).to_broadcast([P, BATCH, DIM])
                pool.tensor_tensor(g_w[:], g_silu[:], wide(V["gn_w"]), ALU.mult).then_inc(S["g_w_r"], 1)
                pool.tensor_tensor(g_b[:], g_silu[:], wide(V["gn_b"]), ALU.mult).then_inc(S["g_b_r"], 1)

            def group_norm(p):
                pool.wait_ge(S["y_rstd_r"], p + 1)
                pool.wait_ge(S["y_w_r"], p + 1)
                pool.tensor_tensor(y_norm[:], y_w[:], spread(y_rstd[:], BATCH * HEADS, HEAD), ALU.mult).then_inc(S["y_norm_r"], 1)

            def group_out(p):
                pool.wait_ge(S["y_norm_r"], p + 1)
                pool.wait_ge(S["g_b_r"], p + 1)
                pool.wait_ge(S["y_w_r"], p + 1)
                pool.tensor_tensor(gated_y[:].rearrange("p b d -> p (b d)"), y_norm[:].rearrange("p g d -> p (g d)"),
                                   g_b[:].rearrange("p b d -> p (b d)"), ALU.add).then_inc(S["gated_y_r"], 1)

            def residual1(p):
                pool.wait_ge(S["update_r"], p + 1)
                pool.tensor_tensor(both(out_sb, p), update[:], both(x1_sb, p), ALU.add).then_inc(S["out_r"], 1)

            def step(s):
                z, a, b, c, d = s + 1, s, s - 1, s - 2, s - 3
                if live(d) and not last(d):
                    group_norm(d)
                if live(z):
                    inverse_root(z, moments0, var0, rstd0, 0)
                if live(b) and not first(b):
                    norm1_low(b)
                if live(a):
                    gate0(a)
                if live(d) and not last(d):
                    group_out(d)
                if live(c):
                    gate_affine(c)
                if first(c):
                    weights_low(("down",))
                if live(b):
                    rotate(b)
                if live(a):
                    inverse_root(a, moments1, var1, rstd1, 1)
                if first(b):
                    weights_low(("qk", "g_logit"))
                if live(d) and not last(d):
                    residual1(d)
                if live(c) and not last(c):
                    group_root(c)

            all_steps(pool, step)


def kernel(L0_attn_seq, L0_attn_W_delta, L0_attn_b_delta, L0_attn_W_value, L0_attn_b_value, L0_ffn_weight,
           L0_ffn_alpha, L0_ffn_bias, L1_attn_W_Q, L1_attn_W_K, L1_attn_W_V, L1_attn_W_G, L1_attn_W_O,
           L1_attn_gn_weight, L1_attn_gn_bias, L1_ffn_w_gate, L1_ffn_w_noise, L1_ffn_Wd, L1_ffn_bd, L1_ffn_Wu,
           L1_ffn_bu):
    import concourse.bacc as bacc
    from concourse.bass_utils import run_bass_kernel_spmd

    heads = lambda w: np.asarray(w).transpose(1, 0, 2).reshape(DIM, DIM)
    rows = lambda v: np.broadcast_to(np.asarray(v)[None, :], (P, len(v)))
    bu = np.zeros((P, DIM), np.float32)
    bu[:EXPERTS] = L1_ffn_bu
    w0 = np.concatenate([
        np.asarray(L0_attn_W_delta).T, np.asarray(L0_attn_W_value).T, np.asarray(L0_ffn_weight).T,
        np.asarray(L0_attn_b_delta)[:, None], np.asarray(L0_attn_b_value)[:, None],
        np.asarray(L0_ffn_bias)[:, None], rows(L0_ffn_alpha)], axis=1)
    w1 = np.concatenate([
        heads(L1_attn_W_Q), heads(L1_attn_W_K), heads(L1_attn_W_V), L1_attn_W_G, L1_ffn_w_gate, L1_attn_W_O,
        np.asarray(L1_ffn_Wd).transpose(1, 0, 2).reshape(DIM, EXPERTS * NECK),
        np.asarray(L1_ffn_Wu).reshape(DOWN, P, DIM).transpose(1, 0, 2).reshape(P, DOWN * DIM),
        np.asarray(L1_ffn_bd).reshape(DOWN, P).T, bu, rows(L1_attn_gn_weight), rows(L1_attn_gn_bias)], axis=1)
    const, tables = constants()
    nc = bacc.Bacc("TRN2", target_bir_lowering=False, num_devices=1)
    arrays = {"x": np.asarray(L0_attn_seq), "w0": w0, "w1": w1, "const": const, "tables": tables,
              "selector": spread_selector()}
    arrays = {k: np.ascontiguousarray(v) for k, v in arrays.items()}
    args = [nc.dram_tensor(k, v.shape, F32, kind="ExternalInput").ap() for k, v in arrays.items()]
    gate_rows = nc.dram_tensor("gate_rows", (EXPERTS, BATCH * P), F32, kind="Internal").ap()
    out = nc.dram_tensor("out", (BATCH, SEQ, DIM), F32, kind="ExternalOutput").ap()
    two_layers(nc, *args, gate_rows, out)
    r = run_bass_kernel_spmd(nc, [arrays], core_ids=[0])
    return r.results[0]["out"]
```
